# Optimizing a Trainium2 kernel written in Bass

```python
import numpy as np
import jax
import jax.numpy as jnp

def _softmax(x, axis=-1):
    return jax.nn.softmax(x, axis=axis)

def _gelu(x):
    return jax.nn.gelu(x, approximate=True)

def _silu(x):
    return jax.nn.silu(x)

def _sigmoid(x):
    return jax.nn.sigmoid(x)

def _layernorm(x, axis=-1, eps=1e-05):
    m = jnp.mean(x, axis=axis, keepdims=True)
    v = jnp.var(x, axis=axis, keepdims=True)
    return (x - m) / jnp.sqrt(v + eps)

def _scatter_add(tgt, idx, src, axis=0):
    return tgt.at[idx].add(src)

def _segment_sum(src, seg, n):
    return jax.ops.segment_sum(src, seg, n)
kernel_name = 'mk_seq_preln_d1_jaxref_r8_290538'

def setup_inputs(seed: int=0):
    np.random.seed(seed)
    _w = jnp.asarray

    def _L0_attn_setup():
        import jax, jax.numpy as jnp
        import numpy as np
        NUM_HEADS = 16
        EPS = 1e-06

        def _split_heads(t, h):
            b, s, d = t.shape
            return t.reshape(b, s, h, d // h).transpose(0, 2, 1, 3)
        key = jax.random.key(seed)
        ks = jax.random.split(key, 6)
        b, s, d = (4, 512, 128)
        scale = 1.0 / np.sqrt(d)
        return {'x': jax.random.normal(ks[0], (b, s, d), dtype=jnp.float32), 'wq': jax.random.normal(ks[1], (d, d), dtype=jnp.float32) * scale, 'wk': jax.random.normal(ks[2], (d, d), dtype=jnp.float32) * scale, 'wv': jax.random.normal(ks[3], (d, d), dtype=jnp.float32) * scale, 'wo': jax.random.normal(ks[4], (d, d), dtype=jnp.float32) * scale, 'bo': jnp.zeros((d,), dtype=jnp.float32)}
    _L0_attn_in = _L0_attn_setup()

    def _L0_ffn_setup():
        import jax, jax.numpy as jnp
        import numpy as np
        S, B, H, F, E, K = (256, 2, 128, 256, 8, 2)

        def _moe_forward(hidden_states, router_w, w1, b1, w2, b2):
            s, b, h = hidden_states.shape
            T = s * b
            x = hidden_states.reshape(T, h)
            logits = jnp.einsum('th,eh->te', x, router_w)
            topk_logits, topk_idx = jax.lax.top_k(logits, K)
            probs = jax.nn.softmax(topk_logits, axis=-1)
            combine = jnp.zeros((T, E), dtype=x.dtype)
            combine = combine.at[jnp.arange(T)[:, None], topk_idx].add(probs.astype(x.dtype))
            hmid = jnp.einsum('th,efh->etf', x, w1) + b1[:, None, :]
            hmid = jax.nn.gelu(hmid, approximate=False)
            y = jnp.einsum('etf,ehf->eth', hmid, w2) + b2[:, None, :]
            out = jnp.einsum('eth,te->th', y, combine)
            return out.reshape(s, b, h)
        key = jax.random.key(seed)
        ks = jax.random.split(key, 6)
        std = 0.02
        return {'hidden_states': jax.random.normal(ks[0], (S, B, H), dtype=jnp.float32), 'router_w': jax.random.normal(ks[1], (E, H), dtype=jnp.float32) * std, 'w1': jax.random.normal(ks[2], (E, F, H), dtype=jnp.float32) * (1.0 / np.sqrt(H)), 'b1': jnp.zeros((E, F), dtype=jnp.float32), 'w2': jax.random.normal(ks[3], (E, H, F), dtype=jnp.float32) * (1.0 / np.sqrt(F)), 'b2': jnp.zeros((E, H), dtype=jnp.float32)}
    _L0_ffn_in = _L0_ffn_setup()
    _d = {'L0_attn_x': _L0_attn_in['x'], 'L0_attn_wq': _L0_attn_in['wq'], 'L0_attn_wk': _L0_attn_in['wk'], 'L0_attn_wv': _L0_attn_in['wv'], 'L0_attn_wo': _L0_attn_in['wo'], 'L0_attn_bo': _L0_attn_in['bo'], 'L0_ffn_router_w': _L0_ffn_in['router_w'], 'L0_ffn_w1': _L0_ffn_in['w1'], 'L0_ffn_b1': _L0_ffn_in['b1'], 'L0_ffn_w2': _L0_ffn_in['w2'], 'L0_ffn_b2': _L0_ffn_in['b2']}
    _x0 = _d['L0_attn_x']
    _d['L0_attn_x'] = jax.random.normal(jax.random.fold_in(jax.random.key(seed), 1), (4, 1024, 128), dtype=_x0.dtype)
    del _x0
    return _d

def reference(L0_attn_x, L0_attn_wq, L0_attn_wk, L0_attn_wv, L0_attn_wo, L0_attn_bo, L0_ffn_router_w, L0_ffn_w1, L0_ffn_b1, L0_ffn_w2, L0_ffn_b2):

    def _L0_attn_ref(x, wq, wk, wv, wo, bo):
        import jax, jax.numpy as jnp
        import numpy as np
        NUM_HEADS = 16
        EPS = 1e-06

        def _split_heads(t, h):
            b, s, d = t.shape
            return t.reshape(b, s, h, d // h).transpose(0, 2, 1, 3)
        h = NUM_HEADS
        q = _split_heads(x @ wq.T, h)
        k = _split_heads(x @ wk.T, h)
        v = _split_heads(x @ wv.T, h)
        qf = jax.nn.elu(q) + 1.0
        kf = jax.nn.elu(k) + 1.0
        k_sum = jnp.sum(kf, axis=-2)
        denom = jnp.sum(qf * k_sum[:, :, None, :], axis=-1, keepdims=True) + EPS
        kv = jnp.einsum('bhsd,bhse->bhde', kf, v)
        q_kv = jnp.einsum('bhsd,bhde->bhse', qf, kv)
        out = q_kv / denom
        b, _, s, dh = out.shape
        out = out.transpose(0, 2, 1, 3).reshape(b, s, h * dh)
        return out @ wo.T + bo

    def _L0_ffn_ref(hidden_states, router_w, w1, b1, w2, b2):
        import jax, jax.numpy as jnp
        import numpy as np
        S, B, H, F, E, K = (256, 2, 128, 256, 8, 2)

        def _moe_forward(hidden_states, router_w, w1, b1, w2, b2):
            s, b, h = hidden_states.shape
            T = s * b
            x = hidden_states.reshape(T, h)
            logits = jnp.einsum('th,eh->te', x, router_w)
            topk_logits, topk_idx = jax.lax.top_k(logits, K)
            probs = jax.nn.softmax(topk_logits, axis=-1)
            combine = jnp.zeros((T, E), dtype=x.dtype)
            combine = combine.at[jnp.arange(T)[:, None], topk_idx].add(probs.astype(x.dtype))
            hmid = jnp.einsum('th,efh->etf', x, w1) + b1[:, None, :]
            hmid = jax.nn.gelu(hmid, approximate=False)
            y = jnp.einsum('etf,ehf->eth', hmid, w2) + b2[:, None, :]
            out = jnp.einsum('eth,te->th', y, combine)
            return out.reshape(s, b, h)
        return _moe_forward(hidden_states, router_w, w1, b1, w2, b2)
    x = L0_attn_x
    x = x + _L0_attn_ref(_layernorm(x, axis=-1), L0_attn_wq, L0_attn_wk, L0_attn_wv, L0_attn_wo, L0_attn_bo)
    x = x + _L0_ffn_ref(_layernorm(x, axis=-1), L0_ffn_router_w, L0_ffn_w1, L0_ffn_b1, L0_ffn_w2, L0_ffn_b2)
    return x

_drawn_inputs = setup_inputs


def setup_inputs(seed=0):
    import zlib

    import numpy as np

    out = dict(_drawn_inputs(seed))
    spreads = {'L0_attn_bo': (0.0, 0.1), 'L0_ffn_b1': (0.0, 0.1), 'L0_ffn_b2': (0.0, 0.1)}
    factors = {}
    for name, (base, spread) in spreads.items():
        noise = np.random.default_rng([zlib.crc32(name.encode()), seed]).standard_normal(out[name].shape)
        drawn = base * np.exp(spread * noise) if base else spread * noise
        out[name] = jnp.asarray(drawn.astype(out[name].dtype))
    for name, factor in factors.items():
        out[name] = (out[name] * factor).astype(out[name].dtype)
    return out
```

```python
from contextlib import ExitStack

import concourse.bass as bass
from concourse import mybir

P = 128
F32 = mybir.dt.float32
F32R = mybir.dt.float32r
ALU = mybir.AluOpType
ACT = mybir.ActivationFunctionType
AX_X = mybir.AxisListType.X
ds = bass.ds

LN_EPS = 1e-5
DEN_EPS = 1e-6
BELOW_ALL = -3.0e38


def attention_moe_program(nc, x, wqT, wkvT, woT, bo, routerT, w1T, b1T, w2T, b2T, out):
    B, S, D = x.shape
    E = routerT.shape[1]
    F = w1T.shape[1] // E
    FC = F // P
    TPB = S // P
    HALF = TPB // 2
    NH = 16
    DH = D // NH
    HW = HALF * P
    assert D == P and HW == 512 and TPB * E <= P

    with ExitStack() as ctx:
        def sb(name, shape, dt=F32):
            return ctx.enter_context(nc.sbuf_tensor(name, shape, dt))

        def ps(name, shape):
            return ctx.enter_context(nc.psum_tensor(name, shape, F32))

        def sem(name):
            return ctx.enter_context(nc.semaphore(name))

        wq_sb = sb("wq_sb", [P, D])
        wkv_sb = sb("wkv_sb", [P, 2, D])
        wo_sb = sb("wo_sb", [P, D])
        bo_sb = sb("bo_sb", [P, D])
        router_sb = sb("router_sb", [P, E])
        w1_sb = sb("w1_sb", [P, E * F])
        w1_hi = sb("w1_hi", [P, E * F], F32R)
        w1_lo = sb("w1_lo", [P, E * F], F32R)
        b1_sb = sb("b1_sb", [P, E * FC])
        w2_sb = sb("w2_sb", [P, E * FC, D])
        b2_sb = sb("b2_sb", [P, E])
        ident = sb("ident", [P, P])
        head_mask = sb("head_mask", [P, P])
        head_cols = sb("head_cols", [P, NH])
        rank = sb("rank", [P, TPB, E])
        minus_half = sb("minus_half", [P, TPB])

        x_sb = sb("x_sb", [P, B * TPB * D])
        ln1_parts = sb("ln1_parts", [P, TPB, 6])
        ln1_mv = sb("ln1_mv", [P, TPB, 2])
        ln1_ve = sb("ln1_ve", [P, TPB])
        ln1_rstd = sb("ln1_rstd", [P, TPB])
        xn1 = sb("xn1", [P, TPB, D])
        xn1T = sb("xn1T", [P, 2, HW])
        exp_q = sb("exp_q", [P, 2, HW])
        qfT = sb("qfT", [P, 2, HW])
        exp_k = sb("exp_k", [P, 2, HW])
        kf = sb("kf", [P, TPB, D])
        v_ones = sb("v_ones", [P, TPB, D + 4])
        kv_heads = sb("kv_heads", [P, D])
        ksum_heads = sb("ksum_heads", [P, NH])
        den = sb("den", [P, TPB * NH])
        rden = sb("rden", [P, TPB, NH])
        att = sb("att", [P, TPB, D])
        attT = sb("attT", [P, 2, HW])
        ln2_parts = sb("ln2_parts", [P, TPB, 6])
        ln2_mv = sb("ln2_mv", [P, TPB, 2])
        ln2_ve = sb("ln2_ve", [P, TPB])
        ln2_rstd = sb("ln2_rstd", [P, TPB])
        xn2 = sb("xn2", [P, TPB, D])
        xn2T = sb("xn2T", [P, TPB * P])
        xn2_hi = sb("xn2_hi", [P, B * TPB * P], F32R)
        xn2_lo = sb("xn2_lo", [P, B * TPB * P], F32R)
        logits = sb("logits", [P, TPB, E])
        rt_a = sb("rt_a", [P, TPB, E])
        rt_b = sb("rt_b", [P, TPB, E])
        first = sb("first", [P, TPB, E])
        second = sb("second", [P, TPB, E])
        top1 = sb("top1", [P, TPB])
        top2 = sb("top2", [P, TPB])
        best = sb("best", [P, TPB])
        gap = sb("gap", [P, TPB])
        tanh_gap = sb("tanh_gap", [P, TPB])
        prob1 = sb("prob1", [P, TPB])
        prob2 = sb("prob2", [P, TPB])
        combine = sb("combine", [P, TPB, E])
        combineT = sb("combineT", [TPB * E, P])
        combine_all = sb("combine_all", [P, 2, E, HW])
        hidden = sb("hidden", [P, 2, FC, HW])
        scaled = sb("scaled", [P, 2, HW])
        acc = sb("acc", [P, 2, HW])
        combine_dram = nc.dram_tensor("combine_dram", [B * TPB * E, P], F32, kind="Internal").ap()

        work = [ps("work0", [P, 512]), ps("work1", [P, 512])]
        kv_ps = ps("kv_ps", [P, 512])
        h_ps = [[ps(f"h_ps{s}{c}", [P, 512]) for c in range(FC)] for s in range(2)]
        y_ps = ps("y_ps", [P, 512])
        den_ps = kv_ps[:, 256:256 + TPB * NH]
        logit_ps = kv_ps[:, 384:384 + TPB * E]
        combT_ps = kv_ps[0:TPB * E, 0:P]

        NAMES = """w_attn w_moe x_in consts zeros
            split passed
            ln1_parts_done ln1_mv_done ln1_ve_done ln1_rstd_done xn1_done xn1T_ps xn1T_done bo_added
            q_ps exp_q_done exp_q_min qf_done k_ps exp_k_done exp_k_min kf_done v_ps v_done
            kv_sum kv_done num_ps den_done rden_done att_done attT_ps attT_done x1_ps x1_done
            ln2_parts_done ln2_mv_done ln2_ve_done ln2_rstd_done xn2_done xn2T_ps xn2_hi_done xn2T_done xn2_lo_done
            logit_done route gap_done tanh_done combine_done combT_done combT_copied comb_stored comb_in0 comb_in1
            h_done gelu_done y_done scaled_done acc_done outT_done out_done out_stored""".split()
        s = {n: sem(n) for n in NAMES}

        FROM_ONE = ("gelu_done", "y_done", "scaled_done", "acc_done", "out_done")

        def counted(eng, name, n):
            eng.wait_ge(s[name], n + 1)

        def wait_apart(eng, name, value):
            eng.wait_ge(s[name], value)
            eng.sem_inc(s["passed"], 1)

        def token_cols(b, j, n):
            return ds((b * TPB + j) * P, n * P)

        x_dram = x.rearrange("b (p j) d -> b p (j d)", j=TPB)
        out_dram = out.rearrange("b (p j) d -> b p (j d)", j=TPB)

        def load_x(sp, b):
            if isinstance(b, int):
                src = x_dram[b]
            else:
                src = x_dram[ds(b, 1)].rearrange("o p n -> (o p) n")
            sp.dma_start(x_sb[:, token_cols(b, 0, TPB)], src).then_inc(s["x_in"], 16)

        def spread_combine(sp, b, half):
            src = combine_dram[ds(b * (TPB * E) + half * HALF * E, HALF * E), :]
            src = src.rearrange("(j e) p -> e j p", e=E)
            for e in range(E):
                sp.dma_start(combine_all[:, half, e, :].rearrange("q (j p) -> q j p", p=P),
                             src[e:e + 1].broadcast_to([P, HALF, P])).then_inc(s[f"comb_in{half}"], 16)

        def store_out(sp, b, half):
            counted(sp, "out_done", b * 2 + half + 1)
            if isinstance(b, int):
                dst = out_dram[b][:, half * HALF * D:(half + 1) * HALF * D]
            else:
                dst = out_dram[ds(b, 1)].rearrange("o p n -> (o p) n")[:, half * HALF * D:(half + 1) * HALF * D]
            sp.dma_start(dst, x_sb[:, token_cols(b, half * HALF, HALF)]).then_inc(s["out_stored"], 16)

        def store_combine(sp, b):
            sp.wait_ge(s["combT_copied"], b + 1)
            sp.dma_start(combine_dram[ds(b * (TPB * E), TPB * E), :], combineT[:, :]).then_inc(s["comb_stored"], 16)
            sp.wait_ge(s["comb_stored"], b * 16 + 16)

        def dve_ln_stats(dve, b, which):
            src_cols = x_sb
            parts, mv = (ln1_parts, ln1_mv) if which == 1 else (ln2_parts, ln2_mv)
            for j in range(TPB):
                last = nc.vector.bn_stats(parts[:, j, :], src_cols[:, token_cols(b, j, 1)])
            last.then_inc(s[f"ln{which}_parts_done"], 1)
            wait_apart(dve, f"ln{which}_parts_done", b + 1)
            for j in range(TPB):
                last = nc.vector.bn_aggr(mv[:, j, :], parts[:, j, :])
            last.then_inc(s[f"ln{which}_mv_done"], 1)

        def pool_rstd(pool, b, which):
            mv, ve, rstd = (ln1_mv, ln1_ve, ln1_rstd) if which == 1 else (ln2_mv, ln2_ve, ln2_rstd)
            wait_apart(pool, f"ln{which}_mv_done", b + 1)
            nc.gpsimd.tensor_scalar(ve[:, :], mv[:, :, 1], LN_EPS, None, ALU.add).then_inc(s[f"ln{which}_ve_done"], 1)
            pool.wait_ge(s[f"ln{which}_ve_done"], b + 1)
            nc.gpsimd.tensor_tensor(rstd[:, :], ve[:, :], minus_half[:, :], ALU.pow).then_inc(s[f"ln{which}_rstd_done"], 1)

        def dve_ln_apply(dve, b, which):
            mv, rstd, xn, done = (ln1_mv, ln1_rstd, xn1, "xn1_done") if which == 1 else (ln2_mv, ln2_rstd, xn2, "xn2_done")
            dve.wait_ge(s[f"ln{which}_rstd_done"], b + 1)
            for j in range(TPB):
                last = nc.vector.tensor_scalar(xn[:, j, :], x_sb[:, token_cols(b, j, 1)], mv[:, j, 0:1], rstd[:, j:j + 1],
                                               ALU.subtract, ALU.mult)
                if j % HALF == HALF - 1:
                    last.then_inc(s[done], 1)

        def pe_transpose_half(dst, src, half):
            for j in range(HALF):
                last = nc.tensor.transpose(dst[:, j * P:(j + 1) * P], src[:, half * HALF + j, :], ident[:, :])
            return last

        class Pe:

            def __init__(self, pe, b):
                self.pe, self.b = pe, b

            def norm1_transposed(self, h):
                pe, b = self.pe, self.b
                pe.wait_ge(s["xn1_done"], b * 2 + h + 1)
                if not isinstance(b, int) or b > 0:
                    pe.wait_ge(s["xn2_lo_done"], b * 2 - 1 + h)
                    pe.wait_ge(s["xn2T_done"], b * 2 - 1 + h)
                pe_transpose_half(work[h], xn1, h).then_inc(s["xn1T_ps"], 1)

            def queries(self, h):
                pe, b = self.pe, self.b
                pe.wait_ge(s["xn1T_done"], b * 2 + h + 1)
                nc.tensor.matmul(work[h][:, :], wq_sb[:, :], xn1T[:, h, :], start=True, stop=True).then_inc(s["q_ps"], 1)

            def keys(self, h):
                pe, b = self.pe, self.b
                pe.wait_ge(s["qf_done"], b * 2 + h + 1)
                for j in range(HALF):
                    last = nc.tensor.matmul(work[h][:, j * P:(j + 1) * P], xn1T[:, h, j * P:(j + 1) * P], wkv_sb[:, 0, :],
                                            start=True, stop=True)
                last.then_inc(s["k_ps"], 1)

            def values(self, h):
                pe, b = self.pe, self.b
                pe.wait_ge(s["kf_done"], b * 2 + h + 1)
                for j in range(HALF):
                    last = nc.tensor.matmul(work[h][:, j * P:(j + 1) * P], xn1T[:, h, j * P:(j + 1) * P], wkv_sb[:, 1, :],
                                            start=True, stop=True)
                last.then_inc(s["v_ps"], 1)

            def kv_sums(self):
                pe, b = self.pe, self.b
                pe.wait_ge(s["v_done"], b * 2 + 2)
                if not isinstance(b, int) or b > 0:
                    pe.wait_ge(s["combT_copied"], b)
                for j in range(TPB):
                    last = nc.tensor.matmul(kv_ps[:, 0:D + 1], kf[:, j, :], v_ones[:, j, 0:D + 1],
                                            start=(j == 0), stop=(j == TPB - 1))
                last.then_inc(s["kv_sum"], 1)

            def numerators(self, h):
                pe, b = self.pe, self.b
                pe.wait_ge(s["kv_done"], b + 1)
                for j in range(HALF):
                    t = h * HALF + j
                    q = qfT[:, h, j * P:(j + 1) * P]
                    nc.tensor.matmul(den_ps[:, t * NH:(t + 1) * NH], q, ksum_heads[:, :], start=True, stop=True)
                    last = nc.tensor.matmul(work[h][:, j * P:(j + 1) * P], q, kv_heads[:, :], start=True, stop=True)
                last.then_inc(s["num_ps"], 1)

            def att_transposed(self, h):
                pe, b = self.pe, self.b
                pe.wait_ge(s["att_done"], b * 2 + h + 1)
                pe_transpose_half(work[h], att, h).then_inc(s["attT_ps"], 1)

            def out_projection(self, h):
                pe, b = self.pe, self.b
                pe.wait_ge(s["attT_done"], b * 2 + h + 1)
                for j in range(HALF):
                    last = nc.tensor.matmul(work[h][:, j * P:(j + 1) * P], attT[:, h, j * P:(j + 1) * P], wo_sb[:, :],
                                            start=True, stop=True)
                last.then_inc(s["x1_ps"], 1)

            def norm2_transposed(self, h):
                pe, b = self.pe, self.b
                pe.wait_ge(s["xn2_done"], b * 2 + h + 1)
                pe_transpose_half(work[h], xn2, h).then_inc(s["xn2T_ps"], 1)

            def router(self):
                pe, b = self.pe, self.b
                pe.wait_ge(s["xn2T_done"], b * 2 + 2)
                for t in range(TPB):
                    last = nc.tensor.matmul(logit_ps[:, t * E:(t + 1) * E], xn2T[:, t * P:(t + 1) * P], router_sb[:, :],
                                            start=True, stop=True)
                last.then_inc(s["logit_done"], 1)

            def combine_transposed(self):
                pe, b = self.pe, self.b
                wait_apart(pe, "combine_done", b + 1)
                nc.tensor.transpose(combT_ps, combine[:, :, :].rearrange("p j e -> p (j e)"), ident[:, :])\
                    .then_inc(s["combT_done"], 1)

        class Act:

            def __init__(self, act, b):
                self.act, self.b = act, b

            def norm1_copy(self, h):
                self.act.wait_ge(s["xn1T_ps"], self.b * 2 + h + 1)
                nc.scalar.activation(xn1T[:, h, :], work[h][:, :], ACT.Copy).then_inc(s["xn1T_done"], 1)

            def exp_queries(self, h):
                self.act.wait_ge(s["q_ps"], self.b * 2 + h + 1)
                nc.scalar.activation(exp_q[:, h, :], work[h][:, :], ACT.Exp).then_inc(s["exp_q_done"], 1)

            def exp_keys(self, h):
                self.act.wait_ge(s["k_ps"], self.b * 2 + h + 1)
                nc.scalar.activation(exp_k[:, h, :], work[h][:, :], ACT.Exp).then_inc(s["exp_k_done"], 1)

            def values_copy(self, h):
                self.act.wait_ge(s["v_ps"], self.b * 2 + h + 1)
                nc.scalar.activation(v_ones[:, h * HALF:(h + 1) * HALF, 0:D],
                                     work[h][:, :].rearrange("p (j d) -> p j d", d=D), ACT.Copy).then_inc(s["v_done"], 1)

            def att_copy(self, h):
                self.act.wait_ge(s["attT_ps"], self.b * 2 + h + 1)
                nc.scalar.activation(attT[:, h, :], work[h][:, :], ACT.Copy).then_inc(s["attT_done"], 1)

            def norm2_copies(self, h):
                self.act.wait_ge(s["xn2T_ps"], self.b * 2 + h + 1)
                nc.scalar.activation(xn2_hi[:, token_cols(self.b, h * HALF, HALF)], work[h][:, :], ACT.Copy)\
                    .then_inc(s["xn2_hi_done"], 1)
                nc.scalar.activation(xn2T[:, h * HW:(h + 1) * HW], work[h][:, :], ACT.Copy).then_inc(s["xn2T_done"], 1)

            def tanh(self):
                self.act.wait_ge(s["gap_done"], self.b + 1)
                nc.scalar.activation(tanh_gap[:, :], gap[:, :], ACT.Tanh, scale=0.5).then_inc(s["tanh_done"], 1)

            def combine_copy(self):
                self.act.wait_ge(s["combT_done"], self.b + 1)
                if not isinstance(self.b, int) or self.b > 0:
                    self.act.wait_ge(s["comb_stored"], self.b * 16)
                nc.scalar.activation(combineT[:, :], combT_ps, ACT.Copy).then_inc(s["combT_copied"], 1)

        def pool_clamp(pool, b, which, h):
            buf = exp_q if which == "q" else exp_k
            wait_apart(pool, f"exp_{which}_done", b * 2 + h + 1)
            nc.gpsimd.tensor_scalar(buf[:, h, :], buf[:, h, :], 1.0, None, ALU.min).then_inc(s[f"exp_{which}_min"], 1)

        def pool_add_bo(pool, b):
            pool.wait_ge(s["xn1_done"], b * 2 + 2)
            for j in range(TPB):
                cols = x_sb[:, token_cols(b, j, 1)]
                last = nc.gpsimd.tensor_tensor(cols, cols, bo_sb[:, :], ALU.add)
            last.then_inc(s["bo_added"], 1)

        def dve_features(dve, b, which, h):
            buf, dst, done = (exp_q, qfT[:, h, :], "qf_done") if which == "q" else (exp_k, kf[:, h * HALF:(h + 1) * HALF, :], "kf_done")
            dve.wait_ge(s[f"exp_{which}_min"], b * 2 + h + 1)
            src, e = work[h][:, :], buf[:, h, :]
            if which == "k":
                dst = dst.rearrange("p j d -> p (j d)")
            nc.vector.scalar_tensor_tensor(dst, src, 0.0, e, ALU.max, ALU.add).then_inc(s[done], 1)

        def dve_kv(dve, b):
            dve.wait_ge(s["kv_sum"], b + 1)
            nc.vector.tensor_tensor(kv_heads[:, :], kv_ps[:, 0:D], head_mask[:, :], ALU.mult)
            nc.vector.tensor_scalar(ksum_heads[:, :], head_cols[:, :], kv_ps[:, D:D + 1], None, ALU.mult).then_inc(s["kv_done"], 1)

        def dve_den(dve, b):
            dve.wait_ge(s["num_ps"], b * 2 + 2)
            nc.vector.tensor_scalar(den[:, :], den_ps, DEN_EPS, None, ALU.add).then_inc(s["den_done"], 1)
            dve.wait_ge(s["den_done"], b + 1)
            nc.vector.reciprocal(rden[:, :, :].rearrange("p j n -> p (j n)"), den[:, :]).then_inc(s["rden_done"], 1)
            dve.wait_ge(s["rden_done"], b + 1)

        def dve_att(dve, b, h):
            r = rden[:, h * HALF:(h + 1) * HALF, :].rearrange("p j n -> p (j n)").unsqueeze(2).broadcast_to([P, HALF * NH, DH])
            nc.vector.tensor_tensor(att[:, h * HALF:(h + 1) * HALF, :].rearrange("p j (n e) -> p (j n) e", e=DH),
                                    work[h][:, :].rearrange("p (m e) -> p m e", e=DH), r, ALU.mult).then_inc(s["att_done"], 1)

        def dve_x1(dve, b, h):
            dve.wait_ge(s["x1_ps"], b * 2 + h + 1)
            if h == 0:
                dve.wait_ge(s["bo_added"], b + 1)
            cols = x_sb[:, token_cols(b, h * HALF, HALF)]
            nc.vector.tensor_tensor(cols, work[h][:, :], cols, ALU.add).then_inc(s["x1_done"], 1)

        def dve_norm2_lo(dve, b, h):
            cols = token_cols(b, h * HALF, HALF)
            dve.wait_ge(s["xn2T_done"], b * 2 + h + 1)
            nc.vector.tensor_tensor(xn2_lo[:, cols], work[h][:, :], xn2_hi[:, cols].bitcast(F32), ALU.subtract)\
                .then_inc(s["xn2_lo_done"], 1)

        ROUTE = 14

        def dve_route(dve, b):
            count = [0]

            def landed(ins):
                count[0] += 1
                ins.then_inc(s["route"], 1)
                dve.wait_ge(s["route"], b * ROUTE + count[0])

            def over_experts(a):
                return a[:, :].unsqueeze(2).broadcast_to([P, TPB, E])

            V = nc.vector
            dve.wait_ge(s["logit_done"], b + 1)
            landed(V.tensor_copy(logits[:, :, :].rearrange("p j e -> p (j e)"), logit_ps))

            def choose(values, top, chosen):
                landed(V.reduce_max(top[:, :], values[:, :, :], AX_X))
                landed(V.tensor_tensor(rt_a[:, :, :], values[:, :, :], over_experts(top), ALU.is_equal))
                landed(V.tensor_tensor(rt_a[:, :, :], rt_a[:, :, :], rank[:, :, :], ALU.mult))
                landed(V.reduce_max(best[:, :], rt_a[:, :, :], AX_X))
                landed(V.tensor_tensor(chosen[:, :, :], rt_a[:, :, :], over_experts(best), ALU.is_equal))

            choose(logits, top1, first)
            landed(V.scalar_tensor_tensor(rt_b[:, :, :], first[:, :, :], BELOW_ALL, logits[:, :, :], ALU.mult, ALU.add))
            choose(rt_b, top2, second)
            V.tensor_tensor(gap[:, :], top1[:, :], top2[:, :], ALU.subtract).then_inc(s["gap_done"], 1)
            dve.wait_ge(s["tanh_done"], b + 1)
            V.tensor_scalar(prob1[:, :], tanh_gap[:, :], 0.5, 0.5, ALU.mult, ALU.add)
            landed(V.tensor_scalar(prob2[:, :], tanh_gap[:, :], -0.5, 0.5, ALU.mult, ALU.add))
            V.tensor_tensor(first[:, :, :], first[:, :, :], over_experts(prob1), ALU.mult)
            landed(V.tensor_tensor(second[:, :, :], second[:, :, :], over_experts(prob2), ALU.mult))
            V.tensor_tensor(combine[:, :, :], first[:, :, :], second[:, :, :], ALU.add).then_inc(s["combine_done"], 1)
            assert count[0] == ROUTE

        def pe_hidden(pe, b, h, e):
            n = (b * 2 + h) * E + e
            if e == 0:
                pe.wait_ge(s["xn2_lo_done"], b * 2 + h + 1)
            if h or e or not isinstance(b, int) or b:
                counted(pe, "gelu_done", (n - 1) * FC)
            cols = token_cols(b, h * HALF, HALF)
            for c in range(FC):
                w = slice((e * FC + c) * P, (e * FC + c + 1) * P)
                dst = h_ps[e % 2][c][:, :]
                nc.tensor.matmul(dst, w1_hi[:, w], xn2_hi[:, cols], start=True, stop=False)
                nc.tensor.matmul(dst, w1_lo[:, w], xn2_hi[:, cols], start=False, stop=False)
                nc.tensor.matmul(dst, w1_hi[:, w], xn2_lo[:, cols], start=False, stop=True).then_inc(s["h_done"], 1)

        def act_gelu(act, b, h, e):
            n = (b * 2 + h) * E + e
            if h or e or not isinstance(b, int) or b:
                counted(act, "y_done", n - 1)
            for c in range(FC):
                act.wait_ge(s["h_done"], n * FC + c + 1)
                i = e * FC + c
                nc.scalar.activation(hidden[:, e % 2, c, :], h_ps[e % 2][c][:, :], ACT.Gelu, bias=b1_sb[:, i:i + 1])\
                    .then_inc(s["gelu_done"], 1)

        def pe_output(pe, b, h, e):
            n = (b * 2 + h) * E + e
            counted(pe, "scaled_done", n)
            if h == 1 and e == 1:
                counted(pe, "out_done", b * 2 + 1)
            if h == 0 and e == 0:
                counted(pe, "out_done", b * 2)
            for c in range(FC):
                counted(pe, "gelu_done", n * FC + c + 1)
                last = nc.tensor.matmul(y_ps[:, :], w2_sb[:, e * FC + c, :], hidden[:, e % 2, c, :],
                                        start=(c == 0), stop=(c == FC - 1))
            last.then_inc(s["y_done"], 1)

        def dve_scale(dve, b, h, e):
            n = (b * 2 + h) * E + e
            counted(dve, "y_done", n + 1)
            if e == 0:
                dve.wait_ge(s[f"comb_in{h}"], (b + 1) * E * 16)
            if e in (1, 2) and (h > 0 or not isinstance(b, int) or b > 0):
                counted(dve, "acc_done", (b * 2 + h) * (E - 1))
            if e > 2:
                counted(dve, "acc_done", (b * 2 + h) * (E - 1) + e - 2)
            dst = acc[:, h, :] if e == 0 else scaled[:, e % 2, :]
            nc.vector.scalar_tensor_tensor(dst, y_ps[:, :], b2_sb[:, e:e + 1], combine_all[:, h, e, :], ALU.add, ALU.mult)\
                .then_inc(s["scaled_done"], 1)

        def pool_sum(pool, b, h, e):
            if e == 0:
                return
            counted(pool, "scaled_done", (b * 2 + h) * E + e + 1)
            if e > 1:
                counted(pool, "acc_done", (b * 2 + h) * (E - 1) + e - 1)
            nc.gpsimd.tensor_tensor(acc[:, h, :], acc[:, h, :], scaled[:, e % 2, :], ALU.add).then_inc(s["acc_done"], 1)

        def pe_out_transposed(pe, b, h):
            counted(pe, "acc_done", (b * 2 + h + 1) * (E - 1))
            counted(pe, "scaled_done", (b * 2 + h + 1) * E + 1 - h)
            for j in range(HALF):
                last = nc.tensor.transpose(y_ps[:, j * P:(j + 1) * P], acc[:, h, j * P:(j + 1) * P], ident[:, :])
            last.then_inc(s["outT_done"], 1)

        def dve_out(dve, b, h):
            dve.wait_ge(s["outT_done"], b * 2 + h + 1)
            cols = x_sb[:, token_cols(b, h * HALF, HALF)]
            nc.vector.tensor_tensor(cols, y_ps[:, :], cols, ALU.add).then_inc(s["out_done"], 1)

        block = ctx.enter_context(nc.Block())

        @block.sync
        def _(sp):
            load_x(sp, 0)
            for dst, src in ((wq_sb[:, :], wqT), (wkv_sb[:, :, :].rearrange("p a d -> p (a d)"), wkvT), (wo_sb[:, :], woT),
                             (bo_sb[:, :], bo.rearrange("(o d) -> o d", o=1).broadcast_to([P, D])), (router_sb[:, :], routerT)):
                sp.dma_start(dst, src).then_inc(s["w_attn"], 16)
            sp.dma_start(w1_sb[:, :], w1T).then_inc(s["w_moe"], 16)
            for dst, src in ((b1_sb[:, :], b1T), (w2_sb[:, :, :].rearrange("p a d -> p (a d)"), w2T), (b2_sb[:, :], b2T)):
                sp.dma_start(dst, src).then_inc(s["w_moe"], 16)
            sp.wait_ge(s["x_in"], 16)
            load_x(sp, 1)
            store_combine(sp, 0)
            spread_combine(sp, 0, 0)
            spread_combine(sp, 0, 1)
            with sp.Fori(1, B - 1) as b:
                sp.wait_ge(s["x_in"], b * 16 + 16)
                load_x(sp, b + 1)
                store_combine(sp, b)
                for half in range(2):
                    counted(sp, "scaled_done", ((b - 1) * 2 + half + 1) * E)
                    spread_combine(sp, b, half)
                    store_out(sp, b - 1, half)
            store_combine(sp, B - 1)
            for half in range(2):
                counted(sp, "scaled_done", ((B - 2) * 2 + half + 1) * E)
                spread_combine(sp, B - 1, half)
                store_out(sp, B - 2, half)
            for half in range(2):
                store_out(sp, B - 1, half)
            sp.wait_ge(s["out_stored"], 2 * B * 16)

        @block.gpsimd
        def _(pool):
            g = nc.gpsimd
            pool.sem_inc(s["acc_done"], 1)
            g.memset(ident[:, :], 0.0)
            g.memset(head_mask[:, :], 1.0)
            g.memset(head_cols[:, :], 1.0)
            g.memset(minus_half[:, :], -0.5)
            for e in range(E):
                g.memset(rank[:, :, e], float(E - e))
            g.memset(v_ones[:, :, D:D + 1], 1.0).then_inc(s["zeros"], 1)
            pool.wait_ge(s["zeros"], 1)
            g.affine_select(out=ident[:, :], in_=ident[:, :], compare_op=ALU.not_equal, fill=1.0, base=0,
                            pattern=[[-1, P]], channel_multiplier=1)
            m = head_mask[:, :].rearrange("p (n e) -> p n e", e=DH)
            g.affine_select(out=m, in_=m, compare_op=ALU.is_ge, fill=0.0, base=0,
                            pattern=[[-DH, NH], [0, DH]], channel_multiplier=1)
            g.affine_select(out=head_cols[:, :], in_=head_cols[:, :], compare_op=ALU.is_ge, fill=0.0, base=0,
                            pattern=[[-DH, NH]], channel_multiplier=1).then_inc(s["zeros"], 1)
            pool.wait_ge(s["zeros"], 2)
            g.affine_select(out=m, in_=m, compare_op=ALU.is_ge, fill=0.0, base=DH - 1,
                            pattern=[[DH, NH], [0, DH]], channel_multiplier=-1)
            g.affine_select(out=head_cols[:, :], in_=head_cols[:, :], compare_op=ALU.is_ge, fill=0.0, base=DH - 1,
                            pattern=[[DH, NH]], channel_multiplier=-1).then_inc(s["consts"], 1)

            def experts(b_moe, b_att):
                for i in range(2 * E):
                    if b_att is not None:
                        if i == 0:
                            pool_rstd(pool, b_att, 1)
                        if i == 2:
                            pool_clamp(pool, b_att, "q", 0)
                            pool_clamp(pool, b_att, "q", 1)
                        if i == 4:
                            pool_clamp(pool, b_att, "k", 0)
                            pool_clamp(pool, b_att, "k", 1)
                        if i == 6:
                            pool_add_bo(pool, b_att)
                        if i == 9:
                            pool_rstd(pool, b_att, 2)
                    pool_sum(pool, b_moe, *divmod(i, E))

            pool.wait_ge(s["w_attn"], 80)
            pool_rstd(pool, 0, 1)
            for which in "qk":
                pool_clamp(pool, 0, which, 0)
                pool_clamp(pool, 0, which, 1)
            pool_add_bo(pool, 0)
            pool_rstd(pool, 0, 2)
            with pool.Fori(1, B) as b:
                experts(b - 1, b)
            experts(B - 1, None)

        @block.scalar
        def _(act):
            act.sem_inc(s["gelu_done"], 1)
            act.wait_ge(s["w_moe"], 64)
            nc.scalar.activation(w1_hi[:, :], w1_sb[:, :], ACT.Copy).then_inc(s["split"], 1)

            def experts(b_moe, b_att, more):
                a = Act(act, b_att)
                for i in range(2 * E):
                    if i + 1 < 2 * E:
                        act_gelu(act, b_moe, *divmod(i + 1, E))
                    elif more:
                        act_gelu(act, b_moe + 1, 0, 0)
                    if b_att is None:
                        continue
                    for h in range(2):
                        if i == 1:
                            a.norm1_copy(h)
                        if i == 2:
                            a.exp_queries(h)
                        if i == 4:
                            a.exp_keys(h)
                        if i == 5:
                            a.values_copy(h)
                        if i == 8:
                            a.att_copy(h)
                        if i == 10:
                            a.norm2_copies(h)
                    if i == 12:
                        a.tanh()
                    if i == 13:
                        a.combine_copy()

            a = Act(act, 0)
            for step in (a.norm1_copy, a.exp_queries, a.exp_keys, a.values_copy, a.att_copy, a.norm2_copies):
                step(0)
                step(1)
            a.tanh()
            a.combine_copy()
            act_gelu(act, 0, 0, 0)
            with act.Fori(1, B) as b:
                experts(b - 1, b, True)
            experts(B - 1, None, False)

        @block.vector
        def _(dve):
            def norm2_stats(b):
                wait_apart(dve, "x1_done", b * 2 + 2)
                dve_ln_stats(dve, b, 2)

            def experts(b_moe, b_att):
                for i in range(2 * E):
                    h, e = divmod(i, E)
                    dve_scale(dve, b_moe, h, e)
                    if h == 1 and e == 0:
                        dve_out(dve, b_moe, 0)
                    if b_att is None:
                        continue
                    if i == 0:
                        wait_apart(dve, "x_in", b_att * 16 + 16)
                        dve_ln_stats(dve, b_att, 1)
                        dve_ln_apply(dve, b_att, 1)
                    if i == 3:
                        dve_features(dve, b_att, "q", 0)
                        dve_features(dve, b_att, "q", 1)
                    if i == 4:
                        dve_features(dve, b_att, "k", 0)
                        dve_features(dve, b_att, "k", 1)
                    if i == 6:
                        dve_kv(dve, b_att)
                    if i == 7:
                        dve_den(dve, b_att)
                        dve_att(dve, b_att, 0)
                        dve_att(dve, b_att, 1)
                    if i == 8:
                        dve_x1(dve, b_att, 0)
                        dve_x1(dve, b_att, 1)
                    if i == 9:
                        norm2_stats(b_att)
                        dve_ln_apply(dve, b_att, 2)
                    if i == 10:
                        dve_norm2_lo(dve, b_att, 0)
                        dve_norm2_lo(dve, b_att, 1)
                    if i == 11:
                        dve_route(dve, b_att)
                dve_out(dve, b_moe, 1)

            dve.sem_inc(s["scaled_done"], 1)
            dve.sem_inc(s["out_done"], 1)
            dve.wait_ge(s["consts"], 1)
            dve.wait_ge(s["x_in"], 16)
            dve_ln_stats(dve, 0, 1)
            dve_ln_apply(dve, 0, 1)
            dve.wait_ge(s["split"], 1)
            nc.vector.tensor_tensor(w1_lo[:, :], w1_sb[:, :], w1_hi[:, :].bitcast(F32), ALU.subtract).then_inc(s["split"], 1)
            for which in "qk":
                dve_features(dve, 0, which, 0)
                dve_features(dve, 0, which, 1)
            dve_kv(dve, 0)
            dve_den(dve, 0)
            dve_att(dve, 0, 0)
            dve_att(dve, 0, 1)
            dve_x1(dve, 0, 0)
            dve_x1(dve, 0, 1)
            norm2_stats(0)
            dve_ln_apply(dve, 0, 2)
            dve_norm2_lo(dve, 0, 0)
            dve_norm2_lo(dve, 0, 1)
            dve_route(dve, 0)
            with dve.Fori(1, B) as b:
                experts(b - 1, b)
            experts(B - 1, None)

        @block.tensor
        def _(pe):
            def experts(b_moe, b_att, more):
                a = Pe(pe, b_att)
                for i in range(2 * E):
                    h, e = divmod(i, E)
                    if i + 1 < 2 * E:
                        pe_hidden(pe, b_moe, *divmod(i + 1, E))
                    elif more:
                        pe_hidden(pe, b_moe + 1, 0, 0)
                    if b_att is not None:
                        for g in range(2):
                            if i == 4:
                                a.keys(g)
                            if i == 7:
                                a.numerators(g)
                            if i == 8:
                                a.att_transposed(g)
                        if i == 13:
                            a.combine_transposed()
                    pe_output(pe, b_moe, h, e)
                    if h == 1 and e == 0:
                        pe_out_transposed(pe, b_moe, 0)
                    if b_att is not None:
                        for g in range(2):
                            if i == 1:
                                a.norm1_transposed(g)
                            if i == 2:
                                a.queries(g)
                            if i == 5:
                                a.values(g)
                            if i == 8:
                                a.out_projection(g)
                            if i == 10:
                                a.norm2_transposed(g)
                        if i == 6:
                            a.kv_sums()
                        if i == 11:
                            a.router()
                pe_out_transposed(pe, b_moe, 1)

            pe.sem_inc(s["y_done"], 1)
            pe.wait_ge(s["consts"], 1)
            pe.wait_ge(s["w_attn"], 80)
            a = Pe(pe, 0)
            for step in (a.norm1_transposed, a.queries, a.keys, a.values):
                step(0)
                step(1)
            a.kv_sums()
            for step in (a.numerators, a.att_transposed, a.out_projection, a.norm2_transposed):
                step(0)
                step(1)
            a.router()
            a.combine_transposed()
            pe.wait_ge(s["w_moe"], 64)
            pe.wait_ge(s["split"], 2)
            pe_hidden(pe, 0, 0, 0)
            with pe.Fori(1, B) as b:
                experts(b - 1, b, True)
            experts(B - 1, None, False)


def kernel(L0_attn_x, L0_attn_wq, L0_attn_wk, L0_attn_wv, L0_attn_wo, L0_attn_bo,
           L0_ffn_router_w, L0_ffn_w1, L0_ffn_b1, L0_ffn_w2, L0_ffn_b2):
    import numpy as np
    import concourse.bacc as bacc
    from concourse.bass_utils import run_bass_kernel_spmd

    def c(a):
        return np.ascontiguousarray(a)

    x = np.asarray(L0_attn_x)
    E, F, D = L0_ffn_w1.shape
    FC = F // P
    arrays = {
        "x": c(x),
        "wqT": c(np.asarray(L0_attn_wq).T),
        "wkvT": c(np.concatenate([np.asarray(L0_attn_wk).T, np.asarray(L0_attn_wv).T], axis=1)),
        "woT": c(np.asarray(L0_attn_wo).T),
        "bo": c(L0_attn_bo),
        "routerT": c(np.asarray(L0_ffn_router_w).T),
        "w1T": c(np.asarray(L0_ffn_w1).transpose(2, 0, 1).reshape(D, E * F)),
        "b1T": c(np.asarray(L0_ffn_b1).reshape(E, FC, P).transpose(2, 0, 1).reshape(P, E * FC)),
        "w2T": c(np.asarray(L0_ffn_w2).reshape(E, D, FC, P).transpose(3, 0, 2, 1).reshape(P, E * FC * D)),
        "b2T": c(np.asarray(L0_ffn_b2).T),
    }
    nc = bacc.Bacc("TRN2", target_bir_lowering=False, num_devices=1)
    args = [nc.dram_tensor(f"in_{n}", a.shape, mybir.dt.from_np(a.dtype), kind="ExternalInput").ap()
            for n, a in arrays.items()]
    out = nc.dram_tensor("out", x.shape, F32, kind="ExternalOutput").ap()
    attention_moe_program(nc, *args, out)
    r = run_bass_kernel_spmd(nc, [{f"in_{n}": a for n, a in arrays.items()}], core_ids=[0])
    return r.results[0]["out"]
```

```python
from contextlib import ExitStack

import concourse.bass as bass
from concourse import mybir

P = 128
F32 = mybir.dt.float32
F32R = mybir.dt.float32r
ALU = mybir.AluOpType
ACT = mybir.ActivationFunctionType
AX_X = mybir.AxisListType.X
ds = bass.ds

LN_EPS = 1e-5
DEN_EPS = 1e-6
BELOW_ALL = -3.0e38


def attention_moe_program(nc, x, wqkT, wvT, woT, bo, routerT, w1T, b1T, w2T, b2, out):
    B, S, D = x.shape
    E = routerT.shape[1]
    F = w1T.shape[1] // E
    FC = F // P
    TPB = S // P
    HALF = TPB // 2
    NH = 16
    DH = D // NH
    HW = HALF * P
    STEPS = 2 * E
    DEPTH = 4
    AHEAD = 2
    assert D == P and HW == 512 and TPB * E <= P and TPB == 8

    with ExitStack() as ctx:
        def sb(name, shape, dt=F32):
            return ctx.enter_context(nc.sbuf_tensor(name, shape, dt))

        def ps(name, shape):
            return ctx.enter_context(nc.psum_tensor(name, shape, F32))

        def sem(name):
            return ctx.enter_context(nc.semaphore(name))

        wqk_sb = sb("wqk_sb", [P, 2 * D])
        wv_sb = sb("wv_sb", [P, D])
        wo_sb = sb("wo_sb", [P, D])
        bo_sb = sb("bo_sb", [P, D])
        router_sb = sb("router_sb", [P, E])
        w1_hi = sb("w1_hi", [P, E * F], F32R)
        w1_lo = sb("w1_lo", [P, E * F], F32R)
        b1_sb = sb("b1_sb", [P, E * FC])
        w2_hi = sb("w2_hi", [P, E * F], F32R)
        w2_lo = sb("w2_lo", [P, E * F], F32R)
        b2_sb = sb("b2_sb", [E, D])
        ident = sb("ident", [P, P])
        ones = sb("ones", [P, P])
        head_mask = sb("head_mask", [P, P])
        rank = sb("rank", [P, TPB, E])
        minus_half = sb("minus_half", [P, TPB])

        x_sb = sb("x_sb", [P, B * TPB * D])
        ln1_mean = sb("ln1_mean", [P, B * TPB])
        ln1_rstd = sb("ln1_rstd", [P, B * TPB])
        parts = sb("parts", [P, TPB, 6])
        moments = sb("moments", [P, TPB, 2])
        var_eps = sb("var_eps", [P, TPB])
        xn1 = sb("xn1", [P, TPB, D])
        xn1T = sb("xn1T", [P, 2, HW])
        exp_qk = sb("exp_qk", [P, 2, HW])
        qkf = sb("qkf", [P, TPB, 2, D])
        k_pairs = sb("k_pairs", [P, 2, D])
        k_tiles = sb("k_tiles", [P, D])
        sums = sb("sums", [P, 2, D])
        kvT_heads = sb("kvT_heads", [P, D])
        w_batch = sb("w_batch", [P, D])
        q_ksum = exp_qk
        den = sb("den", [P, TPB * NH])
        rden = sb("rden", [P, TPB * NH])
        qs = sb("qs", [P, TPB, D])
        qsT = xn1T
        ln2_rstd = sb("ln2_rstd", [P, TPB])
        xn2 = qs
        xn2T = sb("xn2T", [P, TPB * P])
        xn2_hi = sb("xn2_hi", [P, B * TPB * P], F32R)
        xn2_lo = sb("xn2_lo", [P, B * TPB * P], F32R)
        logits = sb("logits", [P, TPB, E])
        rt_a = sb("rt_a", [P, TPB, E])
        rt_b = sb("rt_b", [P, TPB, E])
        first = sb("first", [P, TPB, E])
        second = sb("second", [P, TPB, E])
        top1 = sb("top1", [P, TPB])
        top2 = sb("top2", [P, TPB])
        best = sb("best", [P, TPB])
        gap = sb("gap", [P, TPB])
        tanh_gap = sb("tanh_gap", [P, TPB])
        prob1 = sb("prob1", [P, TPB])
        prob2 = sb("prob2", [P, TPB])
        combine = sb("combine", [P, 2, E, HALF])
        combineT = sb("combineT", [TPB * E, P])
        combine_all = sb("combine_all", [P, 2, E, HW])
        hidden = sb("hidden", [P, DEPTH, FC, HW])
        hidden_hi = sb("hidden_hi", [P, DEPTH, FC, HW], F32R)
        hidden_lo_sb = sb("hidden_lo", [P, DEPTH, FC, HW], F32R)
        combine_rows = sb("combine_rows", [E, 2, HW])
        y_sb = sb("y_sb", [P, HW])
        w1_sb = combine_all[:, 0, 0:4, :].rearrange("p e t -> p (e t)")
        w2_sb = combine_all[:, 1, 0:4, :].rearrange("p e t -> p (e t)")
        combine_dram = nc.dram_tensor("combine_dram", [B * TPB * E, P], F32, kind="Internal").ap()

        work = [ps("work0", [P, 512]), ps("work1", [P, 512])]
        small_ps = ps("small_ps", [P, 512])
        h_ps = [[ps(f"h_ps{s}{c}", [P, 512]) for c in range(FC)] for s in range(2)]
        y_ps = ps("y_ps", [P, 512])
        knT_ps = small_ps[:, 0:D]
        ksum_ps = small_ps[:, D:2 * D]
        kvT_ps = small_ps[:, 2 * D:3 * D]
        w_ps = small_ps[:, 3 * D:4 * D]
        logit_ps = small_ps[:, 384:384 + TPB * E]
        combT_ps = small_ps[0:TPB * E, 0:P]

        NAMES = """w_attn w1_in w2_in w_small consts zeros w1_split w2_split passed
            parts_done moments_done var_done ln1_rstd_done ln1_mean_done xn1_done bo_added
            xn1T_ps xn1T_done qk_ps exp_done clamped qkf_done k_sum_done knT_sum ksum_ps_done sums_done
            kvT_ps_done kvT_done w_ps_done w_done q_ksum_done den_sum den_done rden_done qs_done qsT_ps qsT_done x1_ps x1_done
            ln2_rstd_done xn2_done xn2T_ps xn2T_done xn2_hi_done xn2_lo_done
            logit_done route gap_done tanh_done combine_done combT_done combT_copied comb_stored
            rows_in0 rows_in1
            h_done gelu_done weighted hi_done lo_done lo_done_v y_done y_copied outT_done out_done out_stored""".split()
        s = {n: sem(n) for n in NAMES}
        x_in = [sem(f"x_in{b}") for b in range(B)]
        comb_in = [[sem(f"comb_in{h}{e}") for e in range(E)] for h in range(2)]

        START = {"lo_done": STEPS * FC, "lo_done_v": STEPS, "y_done": DEPTH}

        def start_count(eng, name):
            eng.sem_inc(s[name], START.get(name, 1))

        def counted(eng, name, n):
            eng.wait_ge(s[name], n + START.get(name, 1))

        def wait_apart(eng, name, value):
            eng.wait_ge(s[name], value)
            eng.sem_inc(s["passed"], 1)

        def token_cols(b, j, n):
            return ds((b * TPB + j) * P, n * P)

        def past_first(b):
            return not isinstance(b, int) or b > 0

        x_dram = x.rearrange("b (p j) d -> b p (j d)", j=TPB)
        out_dram = out.rearrange("b (p j) d -> b p (j d)", j=TPB)

        def spread_combine(sp, b, half, e):
            src = combine_dram[ds(b * (TPB * E) + (half * E + e) * HALF, HALF), :]
            sp.dma_start(combine_all[:, half, e, :], src.rearrange("(o j) p -> o (j p)", o=1).broadcast_to([P, HW]))\
                .then_inc(comb_in[half][e], 16)

        def combine_by_expert(sp, b, half):
            src = combine_dram[ds(b * (TPB * E) + half * E * HALF, E * HALF), :]
            sp.dma_start(combine_rows[:, half, :], src.rearrange("(e j) p -> e (j p)", j=HALF)).then_inc(s[f"rows_in{half}"], 16)

        def store_out(sp, b, half):
            counted(sp, "out_done", b * 2 + half + 1)
            if isinstance(b, int):
                dst = out_dram[b][:, half * HALF * D:(half + 1) * HALF * D]
            else:
                dst = out_dram[ds(b, 1)].rearrange("o p n -> (o p) n")[:, half * HALF * D:(half + 1) * HALF * D]
            sp.dma_start(dst, x_sb[:, token_cols(b, half * HALF, HALF)]).then_inc(s["out_stored"], 16)

        def store_combine(sp, b):
            sp.wait_ge(s["combT_copied"], b + 1)
            sp.dma_start(combine_dram[ds(b * (TPB * E), TPB * E), :], combineT[:, :]).then_inc(s["comb_stored"], 16)
            sp.wait_ge(s["comb_stored"], b * 16 + 16)

        LN1_USE = [0, 1] + [b + 2 for b in range(2, B)]
        LN2_USE = B + 1

        def dve_stats(b, tiles):
            for j in tiles:
                last = nc.vector.bn_stats(parts[:, j, :], x_sb[:, token_cols(b, j, 1)])
            last.then_inc(s["parts_done"], 1)

        def dve_stats2(dve, b, half):
            if half == 0:
                wait_apart(dve, "x1_done", b * 2 + 2)
            for j in halves[half]:
                last = nc.vector.bn_stats(parts[:, j, :], x_sb[:, token_cols(b, j, 1)])
            if half == 1:
                last.then_inc(s["parts_done"], 1)

        def dve_moments2(dve, b):
            dve_moments(dve, b + LN2_USE, range(TPB))

        def pool_rstd2(pool, b):
            pool_rstd(pool, b + LN2_USE, range(TPB), ln2_rstd[:, :], "ln2_rstd_done")

        def dve_moments(dve, use, tiles):
            wait_apart(dve, "parts_done", use + 1)
            for j in tiles:
                last = nc.vector.bn_aggr(moments[:, j, :], parts[:, j, :])
            last.then_inc(s["moments_done"], 1)

        def pool_rstd(pool, use, tiles, rstd, done):
            t = slice(tiles[0], tiles[-1] + 1)
            wait_apart(pool, "moments_done", use + 1)
            nc.gpsimd.tensor_scalar(var_eps[:, t], moments[:, t, 1], LN_EPS, None, ALU.add).then_inc(s["var_done"], 1)
            pool.wait_ge(s["var_done"], use + 1)
            nc.gpsimd.tensor_tensor(rstd, var_eps[:, t], minus_half[:, t], ALU.pow).then_inc(s[done], 1)

        def dve_norm1(dve, b, half):
            if isinstance(b, int):
                dve.wait_ge(s["ln1_rstd_done"], b + 1)
                dve.wait_ge(s["ln1_mean_done"], b + 1)
            elif half == 0:
                wait_apart(dve, "knT_sum", b * 2)
            for j in range(half * HALF, (half + 1) * HALF):
                t = ds(b * TPB + j, 1)
                last = nc.vector.tensor_scalar(xn1[:, j, :], x_sb[:, token_cols(b, j, 1)], ln1_mean[:, t], ln1_rstd[:, t],
                                               ALU.subtract, ALU.mult)
            last.then_inc(s["xn1_done"], 1)

        def dve_norm2(dve, b, half):
            if isinstance(b, int):
                dve.wait_ge(s["ln2_rstd_done"], half + 1)
            elif half == 0:
                dve.wait_ge(s["ln2_rstd_done"], b + 2)
            for j in range(half * HALF, (half + 1) * HALF):
                last = nc.vector.tensor_scalar(xn2[:, j, :], x_sb[:, token_cols(b, j, 1)], moments[:, j, 0:1],
                                               ln2_rstd[:, j:j + 1], ALU.subtract, ALU.mult)
            last.then_inc(s["xn2_done"], 1)

        def pe_transpose_half(dst, src, half):
            for j in range(HALF):
                last = nc.tensor.transpose(dst[:, j * P:(j + 1) * P], src[:, half * HALF + j, :], ident[:, :])
            return last

        def pe_norm1_transposed(pe, b, h):
            pe.wait_ge(s["xn1_done"], b * 2 + h + 1)
            if past_first(b):
                pe.wait_ge(s["xn2_lo_done"], b * 2 - 1 + h)
            pe_transpose_half(work[h], xn1, h).then_inc(s["xn1T_ps"], 1)

        def qk_bank(b, u):
            if isinstance(b, int):
                return (work[0], work[1], h_ps[0][0], h_ps[0][1])[u]
            return (work[0], work[1], small_ps, work[0])[u]

        def pe_queries_keys(pe, b, u):
            if u % 2 == 0:
                pe.wait_ge(s["xn1T_done"], b * 2 + u // 2 + 1)
            if u < 2:
                pe.wait_ge(s["xn1T_done"], b * 2 + u + 1)
            elif not isinstance(b, int):
                if u == 2:
                    pe.wait_ge(s["combT_copied"], b)
                    counted(pe, "out_done", b * 2 - 2)
                else:
                    pe.wait_ge(s["qkf_done"], b * 4 + 1)
            for i in range(2):
                j = (2 * u + i) % HALF
                last = nc.tensor.matmul(qk_bank(b, u)[:, i * 2 * D:(i + 1) * 2 * D], xn1T[:, u // 2, j * P:(j + 1) * P],
                                        wqk_sb[:, :], start=True, stop=True)
            last.then_inc(s["qk_ps"], 1)

        def pe_key_tokens(pe, b, half):
            pe.wait_ge(s["qkf_done"], b * 4 + half + 3)
            for j in range(half * HALF, (half + 1) * HALF):
                last = nc.tensor.matmul(knT_ps, xn1[:, j, :], qkf[:, j, 1, :], start=(j == 0), stop=(j == TPB - 1))
            last.then_inc(s["knT_sum"], 1)

        def pe_key_sum(pe, b):
            pe.wait_ge(s["k_sum_done"], b * 4 + 4)
            nc.tensor.matmul(ksum_ps, ones[:, :], k_tiles[:, :], start=True, stop=True).then_inc(s["ksum_ps_done"], 1)

        def pe_kvT(pe, b):
            pe.wait_ge(s["sums_done"], b + 1)
            nc.tensor.matmul(kvT_ps, wv_sb[:, :], sums[:, 0, :], start=True, stop=True).then_inc(s["kvT_ps_done"], 1)

        def pe_w(pe, b):
            pe.wait_ge(s["kvT_done"], b + 1)
            nc.tensor.matmul(w_ps, kvT_heads[:, :], wo_sb[:, :], start=True, stop=True).then_inc(s["w_ps_done"], 1)

        def pe_qs_transposed(pe, b, h):
            pe.wait_ge(s["qs_done"], b * 2 + h + 1)
            pe_transpose_half(work[h], qs, h).then_inc(s["qsT_ps"], 1)

        def pe_project(pe, b, h):
            pe.wait_ge(s["qsT_done"], b * 2 + h + 1)
            if h == 0:
                pe.wait_ge(s["w_done"], b + 1)
            for j in range(HALF):
                last = nc.tensor.matmul(work[h][:, j * P:(j + 1) * P], qsT[:, h, j * P:(j + 1) * P], w_batch[:, :],
                                        start=True, stop=True)
            last.then_inc(s["x1_ps"], 1)

        def pe_norm2_transposed(pe, b, h):
            pe.wait_ge(s["xn2_done"], b * 2 + h + 1)
            pe_transpose_half(work[h], xn2, h).then_inc(s["xn2T_ps"], 1)

        def pe_router(pe, b, half):
            if past_first(b) and half == 0:
                counted(pe, "out_done", b * 2 - 1)
            pe.wait_ge(s["xn2T_done"], b * 2 + half + 1)
            for t in halves[half]:
                last = nc.tensor.matmul(logit_ps[:, t * E:(t + 1) * E], xn2T[:, t * P:(t + 1) * P], router_sb[:, :],
                                        start=True, stop=True)
            last.then_inc(s["logit_done"], 1)

        def pe_combine_transposed(pe, b):
            wait_apart(pe, "combine_done", b + 1)
            nc.tensor.transpose(combT_ps, combine[:, :, :, :].rearrange("p h e j -> p (h e j)"), ident[:, :])\
                .then_inc(s["combT_done"], 1)

        def act_norm1_copy(act, b, h):
            act.wait_ge(s["xn1T_ps"], b * 2 + h + 1)
            nc.scalar.activation(xn1T[:, h, :], work[h][:, :], ACT.Copy).then_inc(s["xn1T_done"], 1)

        def act_exp(act, b, u):
            act.wait_ge(s["qk_ps"], b * 4 + u + 1)
            if u >= 2 or past_first(b):
                act.wait_ge(s["qkf_done"], b * 4 + u - 1)
            nc.scalar.activation(exp_qk[:, u % 2, :], qk_bank(b, u)[:, :], ACT.Exp).then_inc(s["exp_done"], 1)

        def act_sums_copy(act, b):
            act.wait_ge(s["ksum_ps_done"], b + 1)
            nc.scalar.activation(sums[:, :, :].rearrange("p a d -> p (a d)"), small_ps[:, 0:2 * D], ACT.Copy)\
                .then_inc(s["sums_done"], 1)

        def act_w_copy(act, b):
            act.wait_ge(s["w_ps_done"], b + 1)
            nc.scalar.activation(w_batch[:, :], w_ps, ACT.Copy).then_inc(s["w_done"], 1)

        def act_qs_copy(act, b, h):
            act.wait_ge(s["qsT_ps"], b * 2 + h + 1)
            nc.scalar.activation(qsT[:, h, :], work[h][:, :], ACT.Copy).then_inc(s["qsT_done"], 1)

        def act_norm2_copy(act, b, h):
            act.wait_ge(s["xn2T_ps"], b * 2 + h + 1)
            nc.scalar.activation(xn2T[:, h * HW:(h + 1) * HW], work[h][:, :], ACT.Copy).then_inc(s["xn2T_done"], 1)

        def act_norm2_hi(act, b, h):
            act.wait_ge(s["xn2T_ps"], b * 2 + h + 1)
            nc.scalar.activation(xn2_hi[:, token_cols(b, h * HALF, HALF)], work[h][:, :], ACT.Copy).then_inc(s["xn2_hi_done"], 1)

        def act_tanh(act, b):
            act.wait_ge(s["gap_done"], b + 1)
            nc.scalar.activation(tanh_gap[:, :], gap[:, :], ACT.Tanh, scale=0.5).then_inc(s["tanh_done"], 1)

        def act_combine_copy(act, b):
            act.wait_ge(s["combT_done"], b + 1)
            if past_first(b):
                act.wait_ge(s["comb_stored"], b * 16)
            nc.scalar.activation(combineT[:, :], combT_ps, ACT.Copy).then_inc(s["combT_copied"], 1)

        def pool_key_sum(pool, b, part):
            u = part + 1
            if u < 4:
                pool.wait_ge(s["qkf_done"], b * 4 + u + 1)
            if u > 1:
                pool.wait_ge(s["k_sum_done"], b * 4 + u - 1)
            if u < 4:
                before = qkf[:, 0:2, 1, :] if u == 1 else k_pairs[:, :, :]
                last = nc.gpsimd.tensor_tensor(k_pairs[:, :, :], before, qkf[:, 2 * u:2 * u + 2, 1, :], ALU.add)
            else:
                last = nc.gpsimd.tensor_tensor(k_tiles[:, :], k_pairs[:, 0, :], k_pairs[:, 1, :], ALU.add)
            last.then_inc(s["k_sum_done"], 1)

        def pool_add_bo(pool, b, half):
            pool.wait_ge(s["xn1_done"], b * 2 + half + 1)
            cols = x_sb[:, token_cols(b, half * HALF, HALF)].rearrange("p (j d) -> p j d", d=D)
            nc.gpsimd.tensor_tensor(cols, cols, bo_sb[:, :].unsqueeze(1).broadcast_to([P, HALF, D]), ALU.add)\
                .then_inc(s["bo_added"], 1)

        def dve_features(dve, b, pair):
            for u in (2 * pair, 2 * pair + 1):
                e = exp_qk[:, u % 2, :]
                dve.wait_ge(s["exp_done"], b * 4 + u + 1)
                nc.vector.tensor_scalar(e, e, 1.0, None, ALU.min).then_inc(s["clamped"], 1)
            for u in (2 * pair, 2 * pair + 1):
                dve.wait_ge(s["clamped"], b * 4 + u + 1)
                nc.vector.scalar_tensor_tensor(qkf[:, 2 * u:2 * u + 2, :, :].rearrange("p j a d -> p (j a d)"),
                                               qk_bank(b, u)[:, :], 0.0, exp_qk[:, u % 2, :], ALU.max, ALU.add)\
                    .then_inc(s["qkf_done"], 1)

        def dve_kvT(dve, b):
            dve.wait_ge(s["kvT_ps_done"], b + 1)
            nc.vector.tensor_tensor(kvT_heads[:, :], kvT_ps, head_mask[:, :], ALU.mult).then_inc(s["kvT_done"], 1)

        def dve_den(dve, b, h):
            if h == 0:
                dve.wait_ge(s["sums_done"], b + 1)
            t = slice(h * HALF, (h + 1) * HALF)
            nc.vector.tensor_tensor(q_ksum[:, h, :].rearrange("p (j d) -> p j d", d=D), qkf[:, t, 0, :],
                                    sums[:, 1, :].unsqueeze(1).broadcast_to([P, HALF, D]), ALU.mult).then_inc(s["q_ksum_done"], 1)
            dve.wait_ge(s["q_ksum_done"], b * 2 + h + 1)
            nc.vector.reduce_sum(den[:, h * HALF * NH:(h + 1) * HALF * NH],
                                 q_ksum[:, h, :].rearrange("p (m e) -> p m e", e=DH), AX_X).then_inc(s["den_sum"], 1)

        def dve_rden(dve, b, h):
            t = slice(h * HALF * NH, (h + 1) * HALF * NH)
            dve.wait_ge(s["den_sum"], b * 2 + h + 1)
            nc.vector.tensor_scalar(den[:, t], den[:, t], DEN_EPS, None, ALU.add).then_inc(s["den_done"], 1)
            dve.wait_ge(s["den_done"], b * 2 + h + 1)
            nc.vector.reciprocal(rden[:, t], den[:, t]).then_inc(s["rden_done"], 1)

        def dve_qs(dve, b, h):
            dve.wait_ge(s["rden_done"], b * 2 + h + 1)
            t = slice(h * HALF, (h + 1) * HALF)
            r = rden[:, h * HALF * NH:(h + 1) * HALF * NH].rearrange("p (j n) -> p j n", n=NH).unsqueeze(3)
            nc.vector.tensor_tensor(qs[:, t, :].rearrange("p j (n e) -> p j n e", e=DH),
                                    qkf[:, t, 0, :].rearrange("p j (n e) -> p j n e", e=DH),
                                    r.broadcast_to([P, HALF, NH, DH]), ALU.mult).then_inc(s["qs_done"], 1)

        def dve_x1(dve, b, h):
            dve.wait_ge(s["x1_ps"], b * 2 + h + 1)
            dve.wait_ge(s["bo_added"], b * 2 + h + 1)
            cols = x_sb[:, token_cols(b, h * HALF, HALF)]
            nc.vector.tensor_tensor(cols, work[h][:, :], cols, ALU.add).then_inc(s["x1_done"], 1)

        def dve_norm2_lo(dve, b, h):
            cols = token_cols(b, h * HALF, HALF)
            dve.wait_ge(s["xn2_hi_done"], b * 2 + h + 1)
            nc.vector.tensor_tensor(xn2_lo[:, cols], work[h][:, :], xn2_hi[:, cols].bitcast(F32), ALU.subtract)\
                .then_inc(s["xn2_lo_done"], 1)

        ROUTE = 14

        def over_experts(a):
            return a[:, :].unsqueeze(2).broadcast_to([P, TPB, E])

        def route_steps(dve, b, done):
            count = [done]

            def landed(ins):
                count[0] += 1
                ins.then_inc(s["route"], 1)
                dve.wait_ge(s["route"], b * ROUTE + count[0])
            return count, landed

        def choose(landed, values, top, chosen):
            V = nc.vector
            landed(V.reduce_max(top[:, :], values[:, :, :], AX_X))
            landed(V.tensor_tensor(rt_a[:, :, :], values[:, :, :], over_experts(top), ALU.is_equal))
            landed(V.tensor_tensor(rt_a[:, :, :], rt_a[:, :, :], rank[:, :, :], ALU.mult))
            landed(V.reduce_max(best[:, :], rt_a[:, :, :], AX_X))
            landed(V.tensor_tensor(chosen[:, :, :], rt_a[:, :, :], over_experts(best), ALU.is_equal))

        def dve_first(dve, b):
            count, landed = route_steps(dve, b, 0)
            V = nc.vector
            dve.wait_ge(s["logit_done"], b * 2 + 2)
            landed(V.tensor_copy(logits[:, :, :].rearrange("p j e -> p (j e)"), logit_ps))
            choose(landed, logits, top1, first)
            assert count[0] == 6

        def dve_second(dve, b):
            count, landed = route_steps(dve, b, 6)
            V = nc.vector
            landed(V.scalar_tensor_tensor(rt_b[:, :, :], first[:, :, :], BELOW_ALL, logits[:, :, :], ALU.mult, ALU.add))
            choose(landed, rt_b, top2, second)
            V.tensor_tensor(gap[:, :], top1[:, :], top2[:, :], ALU.subtract).then_inc(s["gap_done"], 1)
            assert count[0] == ROUTE - 2

        def dve_combine(dve, b):
            count, landed = route_steps(dve, b, ROUTE - 2)
            V = nc.vector
            dve.wait_ge(s["tanh_done"], b + 1)
            V.tensor_scalar(prob1[:, :], tanh_gap[:, :], 0.5, 0.5, ALU.mult, ALU.add)
            landed(V.tensor_scalar(prob2[:, :], tanh_gap[:, :], -0.5, 0.5, ALU.mult, ALU.add))
            V.tensor_tensor(first[:, :, :], first[:, :, :], over_experts(prob1), ALU.mult)
            landed(V.tensor_tensor(second[:, :, :], second[:, :, :], over_experts(prob2), ALU.mult))
            V.tensor_tensor(combine[:, :, :, :].rearrange("p h e j -> p h j e"), *(
                a[:, :, :].rearrange("p (h j) e -> p h j e", h=2) for a in (first, second)), ALU.add).then_inc(s["combine_done"], 1)
            assert count[0] == ROUTE

        def pe_hidden(pe, b, i):
            n = b * STEPS + i
            h, e = divmod(i, E)
            if e == 0:
                pe.wait_ge(s["xn2_lo_done"], b * 2 + h + 1)
            cols = token_cols(b, h * HALF, HALF)
            for c in range(FC):
                if i >= 2 or past_first(b):
                    counted(pe, "gelu_done", (n - 2) * FC + c + 1)
                w = slice((e * FC + c) * P, (e * FC + c + 1) * P)
                dst = h_ps[i % 2][c][:, :]
                nc.tensor.matmul(dst, w1_hi[:, w], xn2_hi[:, cols], start=True, stop=False)
                nc.tensor.matmul(dst, w1_lo[:, w], xn2_hi[:, cols], start=False, stop=False)
                nc.tensor.matmul(dst, w1_hi[:, w], xn2_lo[:, cols], start=False, stop=True).then_inc(s["h_done"], 1)

        def act_gelu(act, b, i):
            n = b * STEPS + i
            for c in range(FC):
                act.wait_ge(s["h_done"], n * FC + c + 1)
                lo_wait(act, b, i - DEPTH, c)
                k = (i % E) * FC + c
                nc.scalar.activation(hidden[:, i % DEPTH, c, :], h_ps[i % 2][c][:, :], ACT.Gelu, bias=b1_sb[:, k:k + 1])\
                    .then_inc(s["gelu_done"], 1)

        def dve_weigh(dve, b, i):
            n = b * STEPS + i
            h, e = divmod(i, E)
            dve.wait_ge(comb_in[h][e], (b + 1) * 16)
            for c in range(FC):
                counted(dve, "gelu_done", n * FC + c + 1)
                part = hidden[:, i % DEPTH, c, :]
                nc.vector.tensor_tensor(part, part, combine_all[:, h, e, :], ALU.mult).then_inc(s["weighted"], 1)

        def act_hidden_hi(act, b, i):
            n = b * STEPS + i
            if i >= DEPTH or past_first(b):
                counted(act, "y_done", n - DEPTH + 1)
            for c in range(FC):
                act.wait_ge(s["weighted"], n * FC + c + 1)
                nc.scalar.activation(hidden_hi[:, i % DEPTH, c, :], hidden[:, i % DEPTH, c, :], ACT.Copy).then_inc(s["hi_done"], 1)

        def lo_wait(eng, b, i, c):
            if not isinstance(b, int) or b > 0 or i >= 0:
                b, i = (b - 1, i + STEPS) if i < 0 else (b, i)
                if c == 1 and i in VECTOR_LO:
                    counted(eng, "lo_done_v", b * len(VECTOR_LO) + sum(k <= i for k in VECTOR_LO))
                else:
                    pool_chunks = sum(not (k % FC == 1 and k // FC in VECTOR_LO) for k in range(i * FC + c + 1))
                    counted(eng, "lo_done", b * (STEPS * FC - len(VECTOR_LO)) + pool_chunks)

        def hidden_lo(eng, engine, b, i, c, done):
            n = b * STEPS + i
            eng.wait_ge(s["hi_done"], n * FC + c + 1)
            engine.tensor_tensor(hidden_lo_sb[:, i % DEPTH, c, :], hidden[:, i % DEPTH, c, :],
                                 hidden_hi[:, i % DEPTH, c, :].bitcast(F32), ALU.subtract).then_inc(s[done], 1)

        def pool_hidden_lo(pool, b, i):
            hidden_lo(pool, nc.gpsimd, b, i, 0, "lo_done")
            if i not in VECTOR_LO:
                hidden_lo(pool, nc.gpsimd, b, i, 1, "lo_done")

        def dve_hidden_lo(dve, b, i):
            if i in VECTOR_LO:
                hidden_lo(dve, nc.vector, b, i, 1, "lo_done_v")

        def pe_output(pe, b, i):
            n = b * STEPS + i
            h, e = divmod(i, E)
            if e == 0:
                counted(pe, "y_copied", b * 2 + h)
            for c in range(FC):
                w = slice((e * FC + c) * P, (e * FC + c + 1) * P)
                pe.wait_ge(s["hi_done"], n * FC + c + 1)
                nc.tensor.matmul(y_ps[:, :], w2_hi[:, w], hidden_hi[:, i % DEPTH, c, :], start=(e == 0 and c == 0), stop=False)
                nc.tensor.matmul(y_ps[:, :], w2_lo[:, w], hidden_hi[:, i % DEPTH, c, :], start=False, stop=False)
            if e == E - 1:
                pe.wait_ge(s[f"rows_in{h}"], (b + 1) * 16)
                nc.tensor.matmul(y_ps[:, :], b2_sb[:, :], combine_rows[:, h, :], start=False, stop=False)
            for c in range(FC):
                w = slice((e * FC + c) * P, (e * FC + c + 1) * P)
                lo_wait(pe, b, i, c)
                last = nc.tensor.matmul(y_ps[:, :], w2_hi[:, w], hidden_lo_sb[:, i % DEPTH, c, :], start=False,
                                        stop=(e == E - 1 and c == FC - 1))
            last.then_inc(s["y_done"], 1)

        def dve_y_copy(dve, b, h):
            counted(dve, "y_done", b * STEPS + (h + 1) * E)
            counted(dve, "outT_done", b * 2 + h)
            nc.vector.tensor_copy(y_sb[:, :], y_ps[:, :]).then_inc(s["y_copied"], 1)

        def pe_out_transposed(pe, b, h):
            counted(pe, "y_copied", b * 2 + h + 1)
            for j in range(HALF):
                last = nc.tensor.transpose(small_ps[:, j * P:(j + 1) * P], y_sb[:, j * P:(j + 1) * P], ident[:, :])
            last.then_inc(s["outT_done"], 1)

        def dve_out(dve, b, h):
            counted(dve, "outT_done", b * 2 + h + 1)
            cols = x_sb[:, token_cols(b, h * HALF, HALF)]
            nc.vector.tensor_tensor(cols, small_ps[:, :], cols, ALU.add).then_inc(s["out_done"], 1)

        def ahead(step, eng, b, i, more):
            if i + AHEAD < STEPS:
                step(eng, b, i + AHEAD)
            elif more:
                step(eng, b + 1, i + AHEAD - STEPS)

        halves = [range(HALF), range(HALF, TPB)]
        def beside(table, now, eng, b):
            if b is not None:
                for piece, places in table:
                    for k, place in enumerate(places):
                        if place == now:
                            piece(eng, b, *([k] if len(places) > 1 else []))

        VECTOR_LO = (3, 15)
        AT = {"y copy": 16, "out transposed": 9, "out add": 8}
        POOL_AT = ((pool_key_sum, (4, 4, 4, 4)), (pool_add_bo, (6, 6)), (pool_rstd2, (16,)))
        ACT_AT = ((act_norm1_copy, (1, 2)), (act_exp, (2, 2, 2, 2)), (act_sums_copy, (6,)), (act_w_copy, (8,)),
                  (act_qs_copy, (10, 10)), (act_norm2_copy, (18, 18)), (act_norm2_hi, (19, 19)), (act_tanh, (22,)),
                  (act_combine_copy, (23,)))
        DVE_AT = ((dve_norm1, (2, 2)), (dve_features, (2, 4)), (dve_den, (5, 8)), (dve_kvT, (6,)), (dve_rden, (8, 9)),
                  (dve_qs, (9, 10)), (dve_x1, (13, 13)), (dve_stats2, (16, 16)), (dve_moments2, (16,)), (dve_norm2, (18, 18)),
                  (dve_norm2_lo, (19, 19)), (dve_first, (21,)), (dve_second, (21,)), (dve_combine, (23,)))
        PE_AT = ((pe_norm1_transposed, (1, 2)), (pe_queries_keys, (2, 2, 2, 3)), (pe_key_tokens, (4, 5)),
                 (pe_key_sum, (6,)), (pe_kvT, (7,)), (pe_w, (9,)), (pe_qs_transposed, (12, 12)), (pe_project, (13, 13)),
                 (pe_norm2_transposed, (18, 18)), (pe_router, (20, 20)), (pe_combine_transposed, (24,)))

        block = ctx.enter_context(nc.Block())

        @block.sync
        def _(sp):
            sp.dma_start(x_sb[:, token_cols(0, 0, TPB)], x_dram[0]).then_inc(x_in[0], 16)
            for dst, src in ((wqk_sb[:, :], wqkT), (wv_sb[:, :], wvT), (wo_sb[:, :], woT), (router_sb[:, :], routerT)):
                sp.dma_start(dst, src).then_inc(s["w_attn"], 16)
            sp.dma_start(w1_sb, w1T).then_inc(s["w1_in"], 16)
            sp.dma_start(x_sb[:, token_cols(1, 0, TPB)], x_dram[1]).then_inc(x_in[1], 16)
            sp.dma_start(w2_sb, w2T).then_inc(s["w2_in"], 16)
            for dst, src in ((bo_sb[:, :], bo.rearrange("(o d) -> o d", o=1).broadcast_to([P, D])), (b1_sb[:, :], b1T),
                             (b2_sb[:, :], b2)):
                sp.dma_start(dst, src).then_inc(s["w_small"], 16)
            for b in range(2, B):
                sp.dma_start(x_sb[:, token_cols(b, 0, TPB)], x_dram[b]).then_inc(x_in[b], 16)
            store_combine(sp, 0)
            sp.wait_ge(s["w1_split"], 2)
            for e in range(E):
                spread_combine(sp, 0, 0, e)
            combine_by_expert(sp, 0, 0)
            sp.wait_ge(s["w2_split"], 2)
            for e in range(E):
                spread_combine(sp, 0, 1, e)
            combine_by_expert(sp, 0, 1)
            with sp.Fori(1, B) as b:
                store_combine(sp, b)
                for half in range(2):
                    for e in range(E):
                        sp.wait_ge(s["weighted"], ((b - 1) * STEPS + half * E + e + 1) * FC)
                        spread_combine(sp, b, half, e)
                    counted(sp, "y_done", (b - 1) * STEPS + (half + 1) * E)
                    combine_by_expert(sp, b, half)
                    store_out(sp, b - 1, half)
            for half in range(2):
                store_out(sp, B - 1, half)
            sp.wait_ge(s["out_stored"], 2 * B * 16)

        @block.gpsimd
        def _(pool):
            g = nc.gpsimd
            start_count(pool, "lo_done")
            start_count(pool, "lo_done_v")
            g.memset(ident[:, :], 0.0)
            g.memset(head_mask[:, :], 1.0)
            g.memset(ones[:, :], 1.0)
            for e in range(E):
                g.memset(rank[:, :, e], float(E - e))
            g.memset(minus_half[:, :], -0.5).then_inc(s["zeros"], 1)
            pool.wait_ge(s["zeros"], 1)
            g.affine_select(out=ident[:, :], in_=ident[:, :], compare_op=ALU.not_equal, fill=1.0, base=0,
                            pattern=[[-1, P]], channel_multiplier=1)
            m = head_mask[:, :].rearrange("p (n e) -> p n e", e=DH)
            g.affine_select(out=m, in_=m, compare_op=ALU.is_ge, fill=0.0, base=0,
                            pattern=[[-DH, NH], [0, DH]], channel_multiplier=1).then_inc(s["zeros"], 1)
            pool.wait_ge(s["zeros"], 2)
            g.affine_select(out=m, in_=m, compare_op=ALU.is_ge, fill=0.0, base=DH - 1,
                            pattern=[[DH, NH], [0, DH]], channel_multiplier=-1).then_inc(s["consts"], 1)

            def lower(whole, hi, lo, split):
                pool.wait_ge(s[split], 1)
                g.tensor_tensor(lo[:, :], whole, hi[:, :].bitcast(F32), ALU.subtract).then_inc(s[split], 1)

            def experts(b, b_att, more):
                for i in range(STEPS):
                    beside(POOL_AT, 2 * i, pool, b_att)
                    ahead(pool_hidden_lo, pool, b, i, more)
                    beside(POOL_AT, 2 * i + 1, pool, b_att)

            def rstd1(b):
                pool_rstd(pool, LN1_USE[b], range(TPB), ln1_rstd[:, b * TPB:(b + 1) * TPB], "ln1_rstd_done")

            rstd1(0)
            lower(w1_sb, w1_hi, w1_lo, "w1_split")
            for part in range(4):
                pool_key_sum(pool, 0, part)
            rstd1(1)
            pool.wait_ge(s["w_small"], 48)
            for half in range(2):
                pool_add_bo(pool, 0, half)
            for h in range(2):
                pool_rstd(pool, 2 + h, halves[h], ln2_rstd[:, h * HALF:(h + 1) * HALF], "ln2_rstd_done")
            lower(w2_sb, w2_hi, w2_lo, "w2_split")
            for b in range(2, B):
                rstd1(b)
            for i in range(AHEAD):
                pool_hidden_lo(pool, 0, i)
            with pool.Fori(1, B) as b:
                experts(b - 1, b, True)
            experts(B - 1, None, False)

        @block.scalar
        def _(act):
            start_count(act, "gelu_done")

            def upper(whole, hi, arrived, split):
                act.wait_ge(s[arrived], 16)
                nc.scalar.activation(hi[:, :], whole, ACT.Copy).then_inc(s[split], 1)

            def experts(b, b_att, more):
                for i in range(STEPS):
                    ahead(act_gelu, act, b, i, more)
                    beside(ACT_AT, 2 * i, act, b_att)
                    ahead(act_hidden_hi, act, b, i, more)
                    beside(ACT_AT, 2 * i + 1, act, b_att)

            upper(w1_sb, w1_hi, "w1_in", "w1_split")
            act_norm1_copy(act, 0, 0)
            act_norm1_copy(act, 0, 1)
            for u in range(4):
                act_exp(act, 0, u)
            upper(w2_sb, w2_hi, "w2_in", "w2_split")
            act_sums_copy(act, 0)
            act_w_copy(act, 0)
            act_qs_copy(act, 0, 0)
            act_qs_copy(act, 0, 1)
            act_norm2_copy(act, 0, 0)
            act_norm2_copy(act, 0, 1)
            act_norm2_hi(act, 0, 0)
            act_norm2_hi(act, 0, 1)
            act.wait_ge(s["w_small"], 48)
            act_gelu(act, 0, 0)
            act_tanh(act, 0)
            act_gelu(act, 0, 1)
            act_combine_copy(act, 0)
            for i in range(AHEAD):
                act_hidden_hi(act, 0, i)
            with act.Fori(1, B) as b:
                experts(b - 1, b, True)
            experts(B - 1, None, False)

        @block.vector
        def _(dve):
            start_count(dve, "y_copied")
            start_count(dve, "out_done")

            def stats1(b):
                dve.wait_ge(x_in[b], 16)
                if LN1_USE[b] > 0:
                    dve.wait_ge(s["moments_done"], LN1_USE[b])
                dve_stats(b, range(TPB))

            def moments1(b):
                if b > 0:
                    dve.wait_ge(s["ln1_rstd_done"], b)
                    dve.wait_ge(s["ln1_mean_done"], b)
                dve_moments(dve, LN1_USE[b], range(TPB))
                dve.wait_ge(s["moments_done"], LN1_USE[b] + 1)
                nc.vector.tensor_copy(ln1_mean[:, b * TPB:(b + 1) * TPB], moments[:, :, 0]).then_inc(s["ln1_mean_done"], 1)

            def experts(b, b_att, more):
                for i in range(STEPS):
                    if 2 * i == AT["y copy"]:
                        dve_y_copy(dve, b, 0)
                    beside(DVE_AT, 2 * i, dve, b_att)
                    ahead(dve_weigh, dve, b, i, more)
                    ahead(dve_hidden_lo, dve, b, i - 1, more)
                    if 2 * i + 1 == AT["y copy"]:
                        dve_y_copy(dve, b, 0)
                    if i == AT["out add"]:
                        dve_out(dve, b, 0)
                    beside(DVE_AT, 2 * i + 1, dve, b_att)
                dve_y_copy(dve, b, 1)
                dve_out(dve, b, 1)

            stats1(0)
            moments1(0)
            for half in range(2):
                dve_norm1(dve, 0, half)
            for pair in range(2):
                dve_features(dve, 0, pair)
            stats1(1)
            moments1(1)
            for h in range(2):
                dve_den(dve, 0, h)
                if h == 0:
                    dve.wait_ge(s["consts"], 1)
                    dve_kvT(dve, 0)
                dve_rden(dve, 0, h)
                dve_qs(dve, 0, h)
            dve.wait_ge(s["ln1_rstd_done"], 2)
            dve.wait_ge(s["ln1_mean_done"], 2)
            for h in range(2):
                dve_x1(dve, 0, h)
                wait_apart(dve, "x1_done", h + 1)
                dve_stats(0, halves[h])
                dve_moments(dve, 2 + h, halves[h])
            for h in range(2):
                dve_norm2(dve, 0, h)
            for h in range(2):
                dve_norm2_lo(dve, 0, h)
            dve_first(dve, 0)
            dve_second(dve, 0)
            dve_combine(dve, 0)
            for b in range(2, B):
                stats1(b)
                moments1(b)
            for i in range(AHEAD):
                dve_weigh(dve, 0, i)
            for i in range(AHEAD - 1):
                dve_hidden_lo(dve, 0, i)
            with dve.Fori(1, B) as b:
                experts(b - 1, b, True)
            experts(B - 1, None, False)

        @block.tensor
        def _(pe):
            start_count(pe, "y_done")
            start_count(pe, "outT_done")

            def experts(b, b_att, more):
                for i in range(STEPS):
                    ahead(pe_hidden, pe, b, i, more)
                    if i == AT["out transposed"]:
                        pe_out_transposed(pe, b, 0)
                    beside(PE_AT, 2 * i, pe, b_att)
                    pe_output(pe, b, i)
                    beside(PE_AT, 2 * i + 1, pe, b_att)
                pe_out_transposed(pe, b, 1)

            pe.wait_ge(s["consts"], 1)
            pe.wait_ge(s["w_attn"], 64)
            pe_norm1_transposed(pe, 0, 0)
            pe_norm1_transposed(pe, 0, 1)
            for u in range(4):
                pe_queries_keys(pe, 0, u)
            pe_key_tokens(pe, 0, 0)
            pe_key_tokens(pe, 0, 1)
            pe_key_sum(pe, 0)
            pe_kvT(pe, 0)
            pe_w(pe, 0)
            pe_qs_transposed(pe, 0, 0)
            pe_project(pe, 0, 0)
            pe_qs_transposed(pe, 0, 1)
            pe_project(pe, 0, 1)
            pe_norm2_transposed(pe, 0, 0)
            pe_norm2_transposed(pe, 0, 1)
            pe_router(pe, 0, 0)
            pe_router(pe, 0, 1)
            pe.wait_ge(s["w1_split"], 2)
            for i in range(AHEAD):
                pe_hidden(pe, 0, i)
            pe.wait_ge(s["w2_split"], 2)
            pe_combine_transposed(pe, 0)
            with pe.Fori(1, B) as b:
                experts(b - 1, b, True)
            experts(B - 1, None, False)


def kernel(L0_attn_x, L0_attn_wq, L0_attn_wk, L0_attn_wv, L0_attn_wo, L0_attn_bo,
           L0_ffn_router_w, L0_ffn_w1, L0_ffn_b1, L0_ffn_w2, L0_ffn_b2):
    import numpy as np
    import concourse.bacc as bacc
    from concourse.bass_utils import run_bass_kernel_spmd

    def c(a):
        return np.ascontiguousarray(a)

    x = np.asarray(L0_attn_x)
    E, F, D = L0_ffn_w1.shape
    FC = F // P
    arrays = {
        "x": c(x),
        "wqkT": c(np.concatenate([np.asarray(L0_attn_wq).T, np.asarray(L0_attn_wk).T], axis=1)),
        "wvT": c(np.asarray(L0_attn_wv).T),
        "woT": c(np.asarray(L0_attn_wo).T),
        "bo": c(L0_attn_bo),
        "routerT": c(np.asarray(L0_ffn_router_w).T),
        "w1T": c(np.asarray(L0_ffn_w1).transpose(2, 0, 1).reshape(D, E * F)),
        "b1T": c(np.asarray(L0_ffn_b1).reshape(E, FC, P).transpose(2, 0, 1).reshape(P, E * FC)),
        "w2T": c(np.asarray(L0_ffn_w2).reshape(E, D, FC, P).transpose(3, 0, 2, 1).reshape(P, E * FC * D)),
        "b2": c(L0_ffn_b2),
    }
    nc = bacc.Bacc("TRN2", target_bir_lowering=False, num_devices=1)
    args = [nc.dram_tensor(f"in_{n}", a.shape, mybir.dt.from_np(a.dtype), kind="ExternalInput").ap()
            for n, a in arrays.items()]
    out = nc.dram_tensor("out", x.shape, F32, kind="ExternalOutput").ap()
    attention_moe_program(nc, *args, out)
    r = run_bass_kernel_spmd(nc, [{f"in_{n}": a for n, a in arrays.items()}], core_ids=[0])
    return r.results[0]["out"]
```

```python
from contextlib import ExitStack

import concourse.bass as bass
from concourse import mybir

P = 128
F32 = mybir.dt.float32
F32R = mybir.dt.float32r
ALU = mybir.AluOpType
ACT = mybir.ActivationFunctionType
AX_X = mybir.AxisListType.X
ds = bass.ds

LN_EPS = 1e-5
DEN_EPS = 1e-6
BELOW_ALL = -3.0e38


def attention_moe_program(nc, x, wqkT, wvT, woT, bo, routerT, w1T, b1T, w2T, b2, out):
    B, S, D = x.shape
    E = routerT.shape[1]
    F = w1T.shape[1] // E
    FC = F // P
    TPB = S // P
    HALF = TPB // 2
    NH = 16
    DH = D // NH
    HW = HALF * P
    STEPS = 2 * E
    DEPTH = 4
    AHEAD = 2
    assert D == P and HW == 512 and TPB * E <= P and TPB == 8

    with ExitStack() as ctx:
        def sb(name, shape, dt=F32):
            return ctx.enter_context(nc.sbuf_tensor(name, shape, dt))

        def ps(name, shape):
            return ctx.enter_context(nc.psum_tensor(name, shape, F32))

        def sem(name):
            return ctx.enter_context(nc.semaphore(name))

        wqk_sb = sb("wqk_sb", [P, 2 * D])
        wv_sb = sb("wv_sb", [P, D])
        wo_sb = sb("wo_sb", [P, D])
        bo_sb = sb("bo_sb", [P, D])
        router_sb = sb("router_sb", [P, E])
        w1_hi = sb("w1_hi", [P, E * F], F32R)
        w1_lo = sb("w1_lo", [P, E * F], F32R)
        b1_sb = sb("b1_sb", [P, E * FC])
        w2_hi = sb("w2_hi", [P, E * F], F32R)
        w2_lo = sb("w2_lo", [P, E * F], F32R)
        b2_sb = sb("b2_sb", [E, D])
        ident = sb("ident", [P, P])
        ones = sb("ones", [P, P])
        head_mask = sb("head_mask", [P, P])
        rank = sb("rank", [P, TPB, E])
        minus_half = sb("minus_half", [P, TPB])

        x_sb = sb("x_sb", [P, B * TPB * D])
        ln1_mean = sb("ln1_mean", [P, B * TPB])
        ln1_rstd = sb("ln1_rstd", [P, B * TPB])
        parts = sb("parts", [P, TPB, 6])
        moments = sb("moments", [P, TPB, 2])
        var_eps = sb("var_eps", [P, TPB])
        xn1 = sb("xn1", [P, TPB, D])
        xn1T = sb("xn1T", [P, 2, HW])
        exp_qk = sb("exp_qk", [P, 2, HW])
        qkf = sb("qkf", [P, TPB, 2, D])
        k_pairs = sb("k_pairs", [P, 2, D])
        k_tiles = sb("k_tiles", [P, D])
        sums = sb("sums", [P, 2, D])
        kvT_heads = sb("kvT_heads", [P, D])
        w_batch = sb("w_batch", [P, D])
        q_ksum = exp_qk
        den = sb("den", [P, TPB * NH])
        rden = sb("rden", [P, TPB * NH])
        qs = sb("qs", [P, TPB, D])
        qsT = xn1T
        ln2_rstd = sb("ln2_rstd", [P, TPB])
        xn2 = qs
        xn2T = sb("xn2T", [P, TPB * P])
        xn2_hi = sb("xn2_hi", [P, B * TPB * P], F32R)
        xn2_lo = sb("xn2_lo", [P, B * TPB * P], F32R)
        logits = sb("logits", [P, TPB, E])
        rt_a = sb("rt_a", [P, TPB, E])
        rt_b = sb("rt_b", [P, TPB, E])
        first = sb("first", [P, TPB, E])
        second = sb("second", [P, TPB, E])
        top1 = sb("top1", [P, TPB])
        top2 = sb("top2", [P, TPB])
        best = sb("best", [P, TPB])
        gap = sb("gap", [P, TPB])
        tanh_gap = sb("tanh_gap", [P, TPB])
        prob1 = sb("prob1", [P, TPB])
        prob2 = sb("prob2", [P, TPB])
        combine = sb("combine", [P, 2, E, HALF])
        combineT = sb("combineT", [TPB * E, P])
        combine_all = sb("combine_all", [P, 2, E, HW])
        hidden = sb("hidden", [P, DEPTH, FC, HW])
        hidden_hi = sb("hidden_hi", [P, DEPTH, FC, HW], F32R)
        hidden_lo_sb = sb("hidden_lo", [P, DEPTH, FC, HW], F32R)
        combine_rows = sb("combine_rows", [E, 2, HW])
        y_sb = sb("y_sb", [P, HW])
        w1_sb = combine_all[:, 0, 0:4, :].rearrange("p e t -> p (e t)")
        w2_sb = combine_all[:, 1, 0:4, :].rearrange("p e t -> p (e t)")
        combine_dram = nc.dram_tensor("combine_dram", [B * TPB * E, P], F32, kind="Internal").ap()

        work = [ps("work0", [P, 512]), ps("work1", [P, 512])]
        small_ps = ps("small_ps", [P, 512])
        h_ps = [[ps(f"h_ps{s}{c}", [P, 512]) for c in range(FC)] for s in range(2)]
        y_ps = ps("y_ps", [P, 512])
        logit_ps = small_ps[:, 384:384 + TPB * E]
        combT_ps = small_ps[0:TPB * E, 0:P]

        NAMES = """w_attn w1_in w2_in w_small consts zeros w1_split w2_split passed
            parts_done moments_done var_done ln1_rstd_done ln1_mean_done xn1_done bo_added
            xn1T_ps xn1T_done qk_ps exp_done clamped qkf_done k_sum_done knT_sum ksum_ps_done sums_done
            kvT_ps_done kvT_done w_ps_done w_done q_ksum_done den_sum den_done rden_done qs_done qsT_ps qsT_done x1_ps x1_done
            ln2_rstd_done xn2_done xn2T_ps xn2T_done xn2_hi_done xn2_lo_done
            logit_done route gap_done tanh_done combine_done comb_ps_done combT_done combT_copied comb_stored
            rows_in0 rows_in1
            h_done gelu_done weighted hi_done lo_done lo_done_v y_done y_copied outT_done out_done out_stored""".split()
        s = {n: sem(n) for n in NAMES}
        x_in = [sem(f"x_in{b}") for b in range(B)]
        x_in0_rest = sem("x_in0_rest")
        comb_in = [[sem(f"comb_in{h}{e}") for e in range(E)] for h in range(2)]

        START = {"lo_done": STEPS * FC, "lo_done_v": STEPS, "y_done": DEPTH}

        def start_count(eng, name):
            eng.sem_inc(s[name], START.get(name, 1))

        def counted(eng, name, n):
            eng.wait_ge(s[name], n + START.get(name, 1))

        def wait_apart(eng, name, value):
            eng.wait_ge(s[name], value)
            eng.sem_inc(s["passed"], 1)

        def token_cols(b, j, n):
            return ds((b * TPB + j) * P, n * P)

        def past_first(b):
            return not isinstance(b, int) or b > 0

        x_dram = x.rearrange("b (p j) d -> b p (j d)", j=TPB)
        out_dram = out.rearrange("b (p j) d -> b p (j d)", j=TPB)

        def spread_combine(sp, b, half, e):
            src = combine_dram[ds(b * (TPB * E) + (half * E + e) * HALF, HALF), :]
            sp.dma_start(combine_all[:, half, e, :], src.rearrange("(o j) p -> o (j p)", o=1).broadcast_to([P, HW]))\
                .then_inc(comb_in[half][e], 16)

        def combine_by_expert(sp, b, half):
            src = combine_dram[ds(b * (TPB * E) + half * E * HALF, E * HALF), :].rearrange("(e j) p -> e (j p)", j=HALF)
            sp.dma_start(combine_rows[:, half, :], src).then_inc(s[f"rows_in{half}"], 16)

        def store_out(sp, b, half):
            counted(sp, "out_done", b * 2 + half + 1)
            if isinstance(b, int):
                dst = out_dram[b][:, half * HALF * D:(half + 1) * HALF * D]
            else:
                dst = out_dram[ds(b, 1)].rearrange("o p n -> (o p) n")[:, half * HALF * D:(half + 1) * HALF * D]
            sp.dma_start(dst, x_sb[:, token_cols(b, half * HALF, HALF)]).then_inc(s["out_stored"], 16)

        def store_combine(sp, b):
            sp.wait_ge(s["combT_copied"], b + 1)
            sp.dma_start(combine_dram[ds(b * (TPB * E), TPB * E), :], combineT[:, :]).then_inc(s["comb_stored"], 16)
            sp.wait_ge(s["comb_stored"], b * 16 + 16)

        LN2_USE = B + 1

        def dve_stats(b, tiles):
            for j in tiles:
                last = nc.vector.bn_stats(parts[:, j, :], x_sb[:, token_cols(b, j, 1)])
            last.then_inc(s["parts_done"], 1)

        def dve_stats2(dve, b, half):
            if half == 0:
                wait_apart(dve, "x1_done", b * 2 + 2)
            for j in halves[half]:
                last = nc.vector.bn_stats(parts[:, j, :], x_sb[:, token_cols(b, j, 1)])
            if half == 1:
                last.then_inc(s["parts_done"], 1)

        def dve_moments2(dve, b):
            wait_apart(dve, "ln1_rstd_done", B)
            dve_moments(dve, b + LN2_USE, range(TPB))

        def pool_rstd2(pool, b):
            pool_rstd(pool, b + LN2_USE, range(TPB), ln2_rstd[:, :], "ln2_rstd_done")

        def dve_moments(dve, use, tiles):
            wait_apart(dve, "parts_done", use + 1)
            for j in tiles:
                last = nc.vector.bn_aggr(moments[:, j, :], parts[:, j, :])
            last.then_inc(s["moments_done"], 1)

        def pool_rstd(pool, use, tiles, rstd, done):
            t = slice(tiles[0], tiles[-1] + 1)
            wait_apart(pool, "moments_done", use + 1)
            nc.gpsimd.tensor_scalar(var_eps[:, t], moments[:, t, 1], LN_EPS, None, ALU.add).then_inc(s["var_done"], 1)
            pool.wait_ge(s["var_done"], use + 1)
            nc.gpsimd.tensor_tensor(rstd, var_eps[:, t], minus_half[:, t], ALU.pow).then_inc(s[done], 1)

        def dve_norm1(dve, b, half):
            if at_start(b):
                dve.wait_ge(s["ln1_rstd_done"], b + 1)
                dve.wait_ge(s["ln1_mean_done"], b + 1)
            if past_first(b) and half == 0:
                wait_apart(dve, "knT_sum", b * 2)
            for j in range(half * HALF, (half + 1) * HALF):
                t = ds(b * TPB + j, 1)
                last = nc.vector.tensor_scalar(xn1[:, j, :], x_sb[:, token_cols(b, j, 1)], ln1_mean[:, t], ln1_rstd[:, t],
                                               ALU.subtract, ALU.mult)
            last.then_inc(s["xn1_done"], 1)

        def dve_norm2(dve, b, half):
            if not past_first(b):
                dve.wait_ge(s["ln2_rstd_done"], half + 1)
            elif half == 0:
                dve.wait_ge(s["ln2_rstd_done"], b + 2)
            for j in range(half * HALF, (half + 1) * HALF):
                last = nc.vector.tensor_scalar(xn2[:, j, :], x_sb[:, token_cols(b, j, 1)], moments[:, j, 0:1],
                                               ln2_rstd[:, j:j + 1], ALU.subtract, ALU.mult)
            last.then_inc(s["xn2_done"], 1)

        def pe_transpose_half(dst, src, half):
            for j in range(HALF):
                last = nc.tensor.transpose(dst[:, j * P:(j + 1) * P], src[:, half * HALF + j, :], ident[:, :])
            return last

        def pe_norm1_transposed(pe, b, h):
            pe.wait_ge(s["xn1_done"], b * 2 + h + 1)
            if not at_start(b):
                pe.wait_ge(s["xn2_lo_done"], b * 2 - 1 + h)
            pe_transpose_half(norm1_bank(b, h), xn1, h).then_inc(s["xn1T_ps"], 1)

        def at_start(b):
            return isinstance(b, int) and b < 2

        def sums_bank(b):
            return y_ps if isinstance(b, int) and b == 1 else small_ps

        def knT_ps(b):
            return sums_bank(b)[:, 0:D]

        def ksum_ps(b):
            return (sums_bank(b) if past_first(b) else y_ps)[:, D:2 * D]

        def kvT_ps(b):
            return sums_bank(b)[:, 2 * D:3 * D]

        def w_ps(b):
            return sums_bank(b)[:, 3 * D:4 * D]

        def norm1_bank(b, h):
            return h_ps[1][h] if isinstance(b, int) and b == 1 else work[h]

        def qk_bank(b, u):
            if at_start(b):
                return (norm1_bank(b, 0), norm1_bank(b, 1), h_ps[0][0], h_ps[0][1])[u]
            return (work[0], work[1], small_ps, work[0])[u]

        def pe_queries_keys(pe, b, u):
            if u % 2 == 0:
                pe.wait_ge(s["xn1T_done"], b * 2 + u // 2 + 1)
            if u < 2:
                pe.wait_ge(s["xn1T_done"], b * 2 + u + 1)
            elif not at_start(b):
                if u == 2:
                    pe.wait_ge(s["combT_copied"], b)
                    counted(pe, "out_done", b * 2 - 3)
                else:
                    pe.wait_ge(s["qkf_done"], b * 4 + 1)
            for i in range(2):
                j = (2 * u + i) % HALF
                last = nc.tensor.matmul(qk_bank(b, u)[:, i * 2 * D:(i + 1) * 2 * D], xn1T[:, u // 2, j * P:(j + 1) * P],
                                        wqk_sb[:, :], start=True, stop=True)
            last.then_inc(s["qk_ps"], 1)

        def pe_key_tokens(pe, b, half):
            if half == 0 and not at_start(b):
                counted(pe, "out_done", b * 2 - 3)
            if at_start(b):
                pe.wait_ge(s["qkf_done"], b * 4 + half * 2 + 2)
            else:
                pe.wait_ge(s["qkf_done"], b * 4 + half + 3)
            for j in range(half * HALF, (half + 1) * HALF):
                if not past_first(b):
                    last = nc.tensor.matmul(ksum_ps(b), ones[:, :], qkf[:, j, 1, :], start=(j == 0), stop=(j == TPB - 1))
                    if j == TPB - 1:
                        last.then_inc(s["ksum_ps_done"], 1)
                last = nc.tensor.matmul(knT_ps(b), xn1[:, j, :], qkf[:, j, 1, :], start=(j == 0), stop=(j == TPB - 1))
            last.then_inc(s["knT_sum"], 1)

        def pe_key_sum(pe, b):
            pe.wait_ge(s["k_sum_done"], b * 4)
            nc.tensor.matmul(ksum_ps(b), ones[:, :], k_tiles[:, :], start=True, stop=True).then_inc(s["ksum_ps_done"], 1)

        def pe_kvT(pe, b):
            pe.wait_ge(s["sums_done"], b + 2)
            nc.tensor.matmul(kvT_ps(b), wv_sb[:, :], sums[:, 0, :], start=True, stop=True).then_inc(s["kvT_ps_done"], 1)

        def pe_w(pe, b):
            pe.wait_ge(s["kvT_done"], b + 1)
            nc.tensor.matmul(w_ps(b), kvT_heads[:, :], wo_sb[:, :], start=True, stop=True).then_inc(s["w_ps_done"], 1)

        def pe_qs_transposed(pe, b, h):
            pe.wait_ge(s["qs_done"], b * 2 + h + 1)
            if past_first(b):
                pe.wait_ge(s["weighted"], (h + 1) * FC)
            pe_transpose_half(work[h], qs, h).then_inc(s["qsT_ps"], 1)

        def pe_project(pe, b, h):
            pe.wait_ge(s["qsT_done"], b * 2 + h + 1)
            if h == 0:
                pe.wait_ge(s["w_done"], b + 1)
            for j in range(HALF):
                last = nc.tensor.matmul(work[h][:, j * P:(j + 1) * P], qsT[:, h, j * P:(j + 1) * P], w_batch[:, :],
                                        start=True, stop=True)
            last.then_inc(s["x1_ps"], 1)

        def pe_norm2_transposed(pe, b, h):
            pe.wait_ge(s["xn2_done"], b * 2 + h + 1)
            pe_transpose_half(work[h], xn2, h).then_inc(s["xn2T_ps"], 1)

        def pe_router(pe, b, half):
            if past_first(b) and half == 0:
                counted(pe, "out_done", b * 2 - 2)
            pe.wait_ge(s["xn2T_done"], b * 2 + half + 1)
            for t in halves[half]:
                last = nc.tensor.matmul(logit_ps[:, t * E:(t + 1) * E], xn2T[:, t * P:(t + 1) * P], router_sb[:, :],
                                        start=True, stop=True)
            last.then_inc(s["logit_done"], 1)

        def pe_combine_transposed(pe, b):
            if past_first(b):
                counted(pe, "out_done", b * 2 - 2)
            wait_apart(pe, "combine_done", b + 1)
            nc.tensor.transpose(combT_ps, combine[:, :, :, :].rearrange("p h e j -> p (h e j)"), ident[:, :])\
                .then_inc(s["combT_done"], 1)

        def act_norm1_copy(act, b, h):
            act.wait_ge(s["xn1T_ps"], b * 2 + h + 1)
            nc.scalar.activation(xn1T[:, h, :], norm1_bank(b, h)[:, :], ACT.Copy).then_inc(s["xn1T_done"], 1)

        def act_exp(act, b, u):
            act.wait_ge(s["qk_ps"], b * 4 + u + 1)
            if u >= 2 or past_first(b):
                act.wait_ge(s["qkf_done"], b * 4 + u - 1)
            nc.scalar.activation(exp_qk[:, u % 2, :], qk_bank(b, u)[:, :], ACT.Exp).then_inc(s["exp_done"], 1)

        def act_sums_copy(act, b):
            act.wait_ge(s["ksum_ps_done"], b + 1)
            if past_first(b):
                act.wait_ge(s["knT_sum"], b * 2 + 2)
                nc.scalar.activation(sums[:, :, :].rearrange("p a d -> p (a d)"), sums_bank(b)[:, 0:2 * D], ACT.Copy)\
                    .then_inc(s["sums_done"], 1)
            else:
                nc.scalar.activation(sums[:, 1, :], ksum_ps(b), ACT.Copy).then_inc(s["sums_done"], 1)
                act.wait_ge(s["knT_sum"], 2)
                nc.scalar.activation(sums[:, 0, :], knT_ps(b), ACT.Copy).then_inc(s["sums_done"], 1)

        def act_w_copy(act, b):
            act.wait_ge(s["w_ps_done"], b + 1)
            nc.scalar.activation(w_batch[:, :], w_ps(b), ACT.Copy).then_inc(s["w_done"], 1)

        def act_qs_copy(act, b, h):
            act.wait_ge(s["qsT_ps"], b * 2 + h + 1)
            nc.scalar.activation(qsT[:, h, :], work[h][:, :], ACT.Copy).then_inc(s["qsT_done"], 1)

        def act_norm2_copy(act, b, h):
            act.wait_ge(s["xn2T_ps"], b * 2 + h + 1)
            nc.scalar.activation(xn2T[:, h * HW:(h + 1) * HW], work[h][:, :], ACT.Copy).then_inc(s["xn2T_done"], 1)

        def act_norm2_hi(act, b, h):
            act.wait_ge(s["xn2T_ps"], b * 2 + h + 1)
            nc.scalar.activation(xn2_hi[:, token_cols(b, h * HALF, HALF)], work[h][:, :], ACT.Copy).then_inc(s["xn2_hi_done"], 1)

        def act_tanh(act, b):
            act.wait_ge(s["gap_done"], b + 1)
            nc.scalar.activation(tanh_gap[:, :], gap[:, :], ACT.Tanh, scale=0.5).then_inc(s["tanh_done"], 1)

        def act_combine_copy(act, b):
            act.wait_ge(s["combT_done"], b + 1)
            if past_first(b):
                act.wait_ge(s["comb_stored"], b * 16)
            nc.scalar.activation(combineT[:, :], combT_ps, ACT.Copy).then_inc(s["combT_copied"], 1)

        def pool_key_sum(pool, b, part):
            u = part + 1
            if u < 4:
                pool.wait_ge(s["qkf_done"], b * 4 + u + 1)
            if u > 1:
                pool.wait_ge(s["k_sum_done"], b * 4 + u - 5)
            if u < 4:
                before = qkf[:, 0:2, 1, :] if u == 1 else k_pairs[:, :, :]
                last = nc.gpsimd.tensor_tensor(k_pairs[:, :, :], before, qkf[:, 2 * u:2 * u + 2, 1, :], ALU.add)
            else:
                last = nc.gpsimd.tensor_tensor(k_tiles[:, :], k_pairs[:, 0, :], k_pairs[:, 1, :], ALU.add)
            last.then_inc(s["k_sum_done"], 1)

        def pool_add_bo(pool, b, half):
            pool.wait_ge(s["xn1_done"], b * 2 + half + 1)
            cols = x_sb[:, token_cols(b, half * HALF, HALF)].rearrange("p (j d) -> p j d", d=D)
            nc.gpsimd.tensor_tensor(cols, cols, bo_sb[:, :].unsqueeze(1).broadcast_to([P, HALF, D]), ALU.add)\
                .then_inc(s["bo_added"], 1)

        def dve_features(dve, b, pair):
            for u in (2 * pair, 2 * pair + 1):
                e = exp_qk[:, u % 2, :]
                dve.wait_ge(s["exp_done"], b * 4 + u + 1)
                nc.vector.tensor_scalar(e, e, 1.0, None, ALU.min).then_inc(s["clamped"], 1)
            for u in (2 * pair, 2 * pair + 1):
                dve.wait_ge(s["clamped"], b * 4 + u + 1)
                nc.vector.scalar_tensor_tensor(qkf[:, 2 * u:2 * u + 2, :, :].rearrange("p j a d -> p (j a d)"),
                                               qk_bank(b, u)[:, :], 0.0, exp_qk[:, u % 2, :], ALU.max, ALU.add)\
                    .then_inc(s["qkf_done"], 1)

        def dve_kvT(dve, b):
            dve.wait_ge(s["kvT_ps_done"], b + 1)
            nc.vector.tensor_tensor(kvT_heads[:, :], kvT_ps(b), head_mask[:, :], ALU.mult).then_inc(s["kvT_done"], 1)

        def dve_den(dve, b, h):
            if h == 0:
                dve.wait_ge(s["sums_done"], b + 2 if past_first(b) else 1)
            t = slice(h * HALF, (h + 1) * HALF)
            nc.vector.tensor_tensor(q_ksum[:, h, :].rearrange("p (j d) -> p j d", d=D), qkf[:, t, 0, :],
                                    sums[:, 1, :].unsqueeze(1).broadcast_to([P, HALF, D]), ALU.mult).then_inc(s["q_ksum_done"], 1)
            dve.wait_ge(s["q_ksum_done"], b * 2 + h + 1)
            nc.vector.reduce_sum(den[:, h * HALF * NH:(h + 1) * HALF * NH],
                                 q_ksum[:, h, :].rearrange("p (m e) -> p m e", e=DH), AX_X).then_inc(s["den_sum"], 1)

        def dve_rden(dve, b, h):
            t = slice(h * HALF * NH, (h + 1) * HALF * NH)
            dve.wait_ge(s["den_sum"], b * 2 + h + 1)
            nc.vector.tensor_scalar(den[:, t], den[:, t], DEN_EPS, None, ALU.add).then_inc(s["den_done"], 1)
            dve.wait_ge(s["den_done"], b * 2 + h + 1)
            nc.vector.reciprocal(rden[:, t], den[:, t]).then_inc(s["rden_done"], 1)

        def dve_qs(dve, b, h):
            dve.wait_ge(s["rden_done"], b * 2 + h + 1)
            t = slice(h * HALF, (h + 1) * HALF)
            r = rden[:, h * HALF * NH:(h + 1) * HALF * NH].rearrange("p (j n) -> p j n", n=NH).unsqueeze(3)
            nc.vector.tensor_tensor(qs[:, t, :].rearrange("p j (n e) -> p j n e", e=DH),
                                    qkf[:, t, 0, :].rearrange("p j (n e) -> p j n e", e=DH),
                                    r.broadcast_to([P, HALF, NH, DH]), ALU.mult).then_inc(s["qs_done"], 1)

        def dve_x1(dve, b, h):
            dve.wait_ge(s["x1_ps"], b * 2 + h + 1)
            dve.wait_ge(s["bo_added"], b * 2 + h + 1)
            cols = x_sb[:, token_cols(b, h * HALF, HALF)]
            nc.vector.tensor_tensor(cols, work[h][:, :], cols, ALU.add).then_inc(s["x1_done"], 1)

        def dve_norm2_lo(dve, b, h):
            cols = token_cols(b, h * HALF, HALF)
            dve.wait_ge(s["xn2_hi_done"], b * 2 + h + 1)
            nc.vector.tensor_tensor(xn2_lo[:, cols], work[h][:, :], xn2_hi[:, cols].bitcast(F32), ALU.subtract)\
                .then_inc(s["xn2_lo_done"], 1)

        ROUTE = 14

        def over_experts(a):
            return a[:, :].unsqueeze(2).broadcast_to([P, TPB, E])

        def route_steps(dve, b, done):
            count = [done]

            def landed(ins):
                count[0] += 1
                ins.then_inc(s["route"], 1)
                dve.wait_ge(s["route"], b * ROUTE + count[0])
            return count, landed

        def choose(landed, values, top, chosen):
            V = nc.vector
            landed(V.reduce_max(top[:, :], values[:, :, :], AX_X))
            landed(V.tensor_tensor(rt_a[:, :, :], values[:, :, :], over_experts(top), ALU.is_equal))
            landed(V.tensor_tensor(rt_a[:, :, :], rt_a[:, :, :], rank[:, :, :], ALU.mult))
            landed(V.reduce_max(best[:, :], rt_a[:, :, :], AX_X))
            landed(V.tensor_tensor(chosen[:, :, :], rt_a[:, :, :], over_experts(best), ALU.is_equal))

        def dve_first(dve, b):
            count, landed = route_steps(dve, b, 0)
            V = nc.vector
            dve.wait_ge(s["logit_done"], b * 2 + 2)
            landed(V.tensor_copy(logits[:, :, :].rearrange("p j e -> p (j e)"), logit_ps))
            choose(landed, logits, top1, first)
            assert count[0] == 6

        def dve_second(dve, b):
            count, landed = route_steps(dve, b, 6)
            V = nc.vector
            landed(V.scalar_tensor_tensor(rt_b[:, :, :], first[:, :, :], BELOW_ALL, logits[:, :, :], ALU.mult, ALU.add))
            choose(landed, rt_b, top2, second)
            V.tensor_tensor(gap[:, :], top1[:, :], top2[:, :], ALU.subtract).then_inc(s["gap_done"], 1)
            assert count[0] == ROUTE - 2

        def dve_combine(dve, b):
            count, landed = route_steps(dve, b, ROUTE - 2)
            V = nc.vector
            dve.wait_ge(s["tanh_done"], b + 1)
            V.tensor_scalar(prob1[:, :], tanh_gap[:, :], 0.5, 0.5, ALU.mult, ALU.add)
            landed(V.tensor_scalar(prob2[:, :], tanh_gap[:, :], -0.5, 0.5, ALU.mult, ALU.add))
            V.tensor_tensor(first[:, :, :], first[:, :, :], over_experts(prob1), ALU.mult)
            landed(V.tensor_tensor(second[:, :, :], second[:, :, :], over_experts(prob2), ALU.mult))
            V.tensor_tensor(combine[:, :, :, :].rearrange("p h e j -> p h j e"), *(
                a[:, :, :].rearrange("p (h j) e -> p h j e", h=2) for a in (first, second)), ALU.add).then_inc(s["combine_done"], 1)
            assert count[0] == ROUTE

        def pe_hidden(pe, b, i):
            n = b * STEPS + i
            h, e = divmod(i, E)
            if e == 0:
                pe.wait_ge(s["xn2_lo_done"], b * 2 + h + 1)
            cols = token_cols(b, h * HALF, HALF)
            for c in range(FC):
                if i >= 2 or past_first(b):
                    counted(pe, "gelu_done", (n - 2) * FC + c + 1)
                w = slice((e * FC + c) * P, (e * FC + c + 1) * P)
                dst = h_ps[i % 2][c][:, :]
                nc.tensor.matmul(dst, w1_hi[:, w], xn2_hi[:, cols], start=True, stop=False)
                nc.tensor.matmul(dst, w1_lo[:, w], xn2_hi[:, cols], start=False, stop=False)
                nc.tensor.matmul(dst, w1_hi[:, w], xn2_lo[:, cols], start=False, stop=True).then_inc(s["h_done"], 1)

        def act_gelu(act, b, i):
            n = b * STEPS + i
            for c in range(FC):
                act.wait_ge(s["h_done"], n * FC + c + 1)
                lo_wait(act, b, i - DEPTH, c)
                k = (i % E) * FC + c
                nc.scalar.activation(hidden[:, i % DEPTH, c, :], h_ps[i % 2][c][:, :], ACT.Gelu, bias=b1_sb[:, k:k + 1])\
                    .then_inc(s["gelu_done"], 1)

        def dve_weigh(dve, b, i):
            n = b * STEPS + i
            h, e = divmod(i, E)
            if by_matmul(b, i):
                dve.wait_ge(s["comb_ps_done"], i + 1)
            else:
                dve.wait_ge(comb_in[h][e], (b + 1 - (h == 0 and e < AHEAD)) * 16)
            weights = work[i] if by_matmul(b, i) else combine_all[:, h, e, :]
            for c in range(FC):
                counted(dve, "gelu_done", n * FC + c + 1)
                part = hidden[:, i % DEPTH, c, :]
                nc.vector.tensor_tensor(part, part, weights[:, :], ALU.mult).then_inc(s["weighted"], 1)

        def act_hidden_hi(act, b, i):
            n = b * STEPS + i
            if i >= DEPTH or past_first(b):
                counted(act, "y_done", n - DEPTH + 1)
            for c in range(FC):
                act.wait_ge(s["weighted"], n * FC + c + 1)
                nc.scalar.activation(hidden_hi[:, i % DEPTH, c, :], hidden[:, i % DEPTH, c, :], ACT.Copy).then_inc(s["hi_done"], 1)

        def by_matmul(b, i):
            return isinstance(b, int) and b == 0 and i < AHEAD

        def pe_spread_combine(pe, e):
            pe.wait_ge(s["combT_copied"], 1)
            pe.wait_ge(s["xn2_lo_done"], 2)
            for j in range(HALF):
                row = e * HALF + j
                last = nc.tensor.matmul(work[e][:, j * P:(j + 1) * P], ident[0:TPB * E, row:row + 1].broadcast_to([TPB * E, P]),
                                        combineT[:, :], start=True, stop=True)
            last.then_inc(s["comb_ps_done"], 1)

        def lo_wait(eng, b, i, c):
            if not isinstance(b, int) or b > 0 or i >= 0:
                b, i = (b - 1, i + STEPS) if i < 0 else (b, i)
                if c == 1 and i in VECTOR_LO:
                    counted(eng, "lo_done_v", b * len(VECTOR_LO) + sum(k <= i for k in VECTOR_LO))
                else:
                    pool_chunks = sum(not (k % FC == 1 and k // FC in VECTOR_LO) for k in range(i * FC + c + 1))
                    counted(eng, "lo_done", b * (STEPS * FC - len(VECTOR_LO)) + pool_chunks)

        def hidden_lo(eng, engine, b, i, c, done):
            n = b * STEPS + i
            eng.wait_ge(s["hi_done"], n * FC + c + 1)
            engine.tensor_tensor(hidden_lo_sb[:, i % DEPTH, c, :], hidden[:, i % DEPTH, c, :],
                                 hidden_hi[:, i % DEPTH, c, :].bitcast(F32), ALU.subtract).then_inc(s[done], 1)

        def pool_hidden_lo(pool, b, i):
            hidden_lo(pool, nc.gpsimd, b, i, 0, "lo_done")
            if i not in VECTOR_LO:
                hidden_lo(pool, nc.gpsimd, b, i, 1, "lo_done")

        def dve_hidden_lo(dve, b, i):
            if i in VECTOR_LO:
                hidden_lo(dve, nc.vector, b, i, 1, "lo_done_v")

        def pe_output(pe, b, i):
            n = b * STEPS + i
            h, e = divmod(i, E)
            if e == 0:
                counted(pe, "y_copied", b * 2 + h)
            for c in range(FC):
                w = slice((e * FC + c) * P, (e * FC + c + 1) * P)
                pe.wait_ge(s["hi_done"], n * FC + c + 1)
                nc.tensor.matmul(y_ps[:, :], w2_hi[:, w], hidden_hi[:, i % DEPTH, c, :], start=(e == 0 and c == 0), stop=False)
                nc.tensor.matmul(y_ps[:, :], w2_lo[:, w], hidden_hi[:, i % DEPTH, c, :], start=False, stop=False)
            if e == E - 1:
                pe.wait_ge(s[f"rows_in{h}"], (b + 1) * 16)
                nc.tensor.matmul(y_ps[:, :], b2_sb[:, :], combine_rows[:, h, :], start=False, stop=False)
            for c in range(FC):
                w = slice((e * FC + c) * P, (e * FC + c + 1) * P)
                lo_wait(pe, b, i, c)
                last = nc.tensor.matmul(y_ps[:, :], w2_hi[:, w], hidden_lo_sb[:, i % DEPTH, c, :], start=False,
                                        stop=(e == E - 1 and c == FC - 1))
            last.then_inc(s["y_done"], 1)

        def dve_y_copy(dve, b, h):
            counted(dve, "y_done", b * STEPS + (h + 1) * E)
            counted(dve, "outT_done", b * 2 + h)
            nc.vector.tensor_copy(y_sb[:, :], y_ps[:, :]).then_inc(s["y_copied"], 1)

        def pe_out_transposed(pe, b, h, b_att, b_next):
            if b_att is not None:
                pe.wait_ge(s["route"], b_att * ROUTE + 1)
            if b_att is not None:
                pe.wait_ge(s["combT_copied"], b_att + 1)
            if h == 1:
                if b_next is not None:
                    pe.wait_ge(s["w_done"], b_next + 1)
                    pe.wait_ge(s["qkf_done"], b_next * 4 + 3)
            counted(pe, "y_copied", b * 2 + h + 1)
            for j in range(HALF):
                last = nc.tensor.transpose(small_ps[:, j * P:(j + 1) * P], y_sb[:, j * P:(j + 1) * P], ident[:, :])
            last.then_inc(s["outT_done"], 1)

        def dve_out(dve, b, h):
            counted(dve, "outT_done", b * 2 + h + 1)
            cols = x_sb[:, token_cols(b, h * HALF, HALF)]
            nc.vector.tensor_tensor(cols, small_ps[:, :], cols, ALU.add).then_inc(s["out_done"], 1)

        def ahead(step, eng, b, i, more):
            if i + AHEAD < STEPS:
                step(eng, b, i + AHEAD)
            elif more:
                step(eng, b + 1, i + AHEAD - STEPS)

        halves = [range(HALF), range(HALF, TPB)]
        VECTOR_LO = (2, 11, 12, 15)

        block = ctx.enter_context(nc.Block())

        @block.sync
        def _(sp):
            def steps(b):
                store_combine(sp, b)
                for half in range(2):
                    for e in range(E):
                        sp.wait_ge(s["weighted"], ((b - 1) * STEPS + half * E + e + 1) * FC)
                        spread_combine(sp, b, half, e)
                    counted(sp, "y_done", (b - 1) * STEPS + (half + 1) * E)
                    combine_by_expert(sp, b, half)
                    store_out(sp, b - 1, half)

            for h in range(2):
                sp.dma_start(x_sb[:, token_cols(0, h * HALF, HALF)], x_dram[0][:, h * HALF * D:(h + 1) * HALF * D])\
                    .then_inc((x_in[0], x_in0_rest)[h], 16)
            for dst, src in ((wqk_sb[:, :], wqkT), (wv_sb[:, :], wvT), (wo_sb[:, :], woT), (router_sb[:, :], routerT)):
                sp.dma_start(dst, src).then_inc(s["w_attn"], 16)
            for b in range(1, B):
                sp.dma_start(x_sb[:, token_cols(b, 0, TPB)], x_dram[b]).then_inc(x_in[b], 16)
            sp.dma_start(w1_sb, w1T).then_inc(s["w1_in"], 16)
            for dst, src in ((bo_sb[:, :], bo.rearrange("(o d) -> o d", o=1).broadcast_to([P, D])), (b1_sb[:, :], b1T),
                             (b2_sb[:, :], b2)):
                sp.dma_start(dst, src).then_inc(s["w_small"], 16)
            sp.dma_start(w2_sb, w2T).then_inc(s["w2_in"], 16)
            store_combine(sp, 0)
            sp.wait_ge(s["w1_split"], 2)
            for e in range(AHEAD, E):
                spread_combine(sp, 0, 0, e)
            combine_by_expert(sp, 0, 0)
            sp.wait_ge(s["w2_split"], 2)
            for e in range(E):
                spread_combine(sp, 0, 1, e)
            combine_by_expert(sp, 0, 1)
            with sp.Fori(1, B - 1) as b:
                steps(b)
            steps(B - 1)
            for half in range(2):
                store_out(sp, B - 1, half)
            sp.wait_ge(s["out_stored"], 2 * B * 16)

        @block.gpsimd
        def _(pool):
            g = nc.gpsimd
            start_count(pool, "lo_done")
            start_count(pool, "lo_done_v")
            g.memset(ident[:, :], 0.0)
            g.memset(head_mask[:, :], 1.0)
            g.memset(ones[:, :], 1.0)
            for e in range(E):
                g.memset(rank[:, :, e], float(E - e))
            g.memset(minus_half[:, :], -0.5).then_inc(s["zeros"], 1)
            pool.wait_ge(s["zeros"], 1)
            g.affine_select(out=ident[:, :], in_=ident[:, :], compare_op=ALU.not_equal, fill=1.0, base=0,
                            pattern=[[-1, P]], channel_multiplier=1)
            m = head_mask[:, :].rearrange("p (n e) -> p n e", e=DH)
            g.affine_select(out=m, in_=m, compare_op=ALU.is_ge, fill=0.0, base=0,
                            pattern=[[-DH, NH], [0, DH]], channel_multiplier=1).then_inc(s["zeros"], 1)
            pool.wait_ge(s["zeros"], 2)
            g.affine_select(out=m, in_=m, compare_op=ALU.is_ge, fill=0.0, base=DH - 1,
                            pattern=[[DH, NH], [0, DH]], channel_multiplier=-1).then_inc(s["consts"], 1)

            def lower(whole, hi, lo, split):
                pool.wait_ge(s[split], 1)
                g.tensor_tensor(lo[:, :], whole, hi[:, :].bitcast(F32), ALU.subtract).then_inc(s[split], 1)

            def experts(b, b_att, b_next, more):
                for i in range(STEPS):
                    if b_att is not None:
                        if i == 4:
                            pool_rstd2(pool, b_att)
                    if b_next is not None:
                        if i == 10:
                            for part in range(4):
                                pool_key_sum(pool, b_next, part)
                        if i == 12:
                            for h in range(2):
                                pool_add_bo(pool, b_next, h)
                    ahead(pool_hidden_lo, pool, b, i, more)

            def rstd1(b):
                pool_rstd(pool, b, range(TPB), ln1_rstd[:, b * TPB:(b + 1) * TPB], "ln1_rstd_done")

            for b in range(3):
                rstd1(b)
            pool.wait_ge(s["w_small"], 48)
            for half in range(2):
                pool_add_bo(pool, 0, half)
            lower(w1_sb, w1_hi, w1_lo, "w1_split")
            rstd1(3)
            for h in range(2):
                pool_rstd(pool, B + h, halves[h], ln2_rstd[:, h * HALF:(h + 1) * HALF], "ln2_rstd_done")
            lower(w2_sb, w2_hi, w2_lo, "w2_split")
            for part in range(4):
                pool_key_sum(pool, 1, part)
            for h in range(2):
                pool_add_bo(pool, 1, h)
            for i in range(AHEAD):
                pool_hidden_lo(pool, 0, i)
            with pool.Fori(1, B - 1) as b:
                experts(b - 1, b, b + 1, True)
            experts(B - 2, B - 1, None, True)
            experts(B - 1, None, None, False)

        @block.scalar
        def _(act):
            start_count(act, "gelu_done")

            def upper(whole, hi, arrived, split):
                act.wait_ge(s[arrived], 16)
                nc.scalar.activation(hi[:, :], whole, ACT.Copy).then_inc(s[split], 1)

            def experts(b, b_att, b_next, more):
                for i in range(STEPS):
                    ahead(act_gelu, act, b, i, more)
                    if b_att is not None:
                        if i == 1:
                            act_qs_copy(act, b_att, 1)
                        if i == 5:
                            for h in range(2):
                                act_norm2_copy(act, b_att, h)
                            for h in range(2):
                                act_norm2_hi(act, b_att, h)
                        if i == 7:
                            act_tanh(act, b_att)
                        if i == 8:
                            act_combine_copy(act, b_att)
                    ahead(act_hidden_hi, act, b, i, more)
                    if b_att is not None:
                        if i == 0:
                            act_qs_copy(act, b_att, 0)
                    if b_next is not None:
                        if i == 9:
                            for h in range(2):
                                act_norm1_copy(act, b_next, h)
                        if i == 10:
                            for u in range(4):
                                act_exp(act, b_next, u)
                        if i == 11:
                            act_sums_copy(act, b_next)
                        if i == 13:
                            act_w_copy(act, b_next)

            act_norm1_copy(act, 0, 0)
            act_norm1_copy(act, 0, 1)
            for u in range(4):
                act_exp(act, 0, u)
            upper(w1_sb, w1_hi, "w1_in", "w1_split")
            act_sums_copy(act, 0)
            upper(w2_sb, w2_hi, "w2_in", "w2_split")
            act_w_copy(act, 0)
            act_qs_copy(act, 0, 0)
            act_qs_copy(act, 0, 1)
            for h in range(2):
                act_norm1_copy(act, 1, h)
            for u in range(2):
                act_exp(act, 1, u)
            act_norm2_copy(act, 0, 0)
            act_norm2_copy(act, 0, 1)
            act_norm2_hi(act, 0, 0)
            act_norm2_hi(act, 0, 1)
            for u in range(2, 4):
                act_exp(act, 1, u)
            act.wait_ge(s["w_small"], 48)
            act_tanh(act, 0)
            act_combine_copy(act, 0)
            act_sums_copy(act, 1)
            act_gelu(act, 0, 0)
            act_gelu(act, 0, 1)
            act_w_copy(act, 1)
            for i in range(AHEAD):
                act_hidden_hi(act, 0, i)
            with act.Fori(1, B - 1) as b:
                experts(b - 1, b, b + 1, True)
            experts(B - 2, B - 1, None, True)
            experts(B - 1, None, None, False)

        @block.vector
        def _(dve):
            start_count(dve, "y_copied")
            start_count(dve, "out_done")

            def stats1(b):
                dve.wait_ge(x_in[b], 16)
                if b > 0:
                    dve.wait_ge(s["moments_done"], b)
                dve_stats(b, range(TPB))

            def moments1(b):
                if b > 0:
                    dve.wait_ge(s["ln1_rstd_done"], b)
                    dve.wait_ge(s["ln1_mean_done"], b)
                dve_moments(dve, b, range(TPB))
                dve.wait_ge(s["moments_done"], b + 1)
                nc.vector.tensor_copy(ln1_mean[:, b * TPB:(b + 1) * TPB], moments[:, :, 0]).then_inc(s["ln1_mean_done"], 1)

            def experts(b, b_att, b_next, more):
                for i in range(STEPS):
                    if i == 8:
                        dve_y_copy(dve, b, 0)
                    if b_att is not None:
                        if i == 3:
                            for h in range(2):
                                dve_x1(dve, b_att, h)
                        if i == 5:
                            dve_moments2(dve, b_att)
                        if i == 8:
                            dve_combine(dve, b_att)
                    if b_next is not None:
                        if i == 9:
                            for h in range(2):
                                dve_norm1(dve, b_next, h)
                        if i == 13:
                            dve_den(dve, b_next, 0)
                            dve_kvT(dve, b_next)
                        if i == 14:
                            for h in range(2):
                                dve_rden(dve, b_next, h)
                    ahead(dve_weigh, dve, b, i, more)
                    ahead(dve_hidden_lo, dve, b, i - 1, more)
                    if i == 10:
                        dve_out(dve, b, 0)
                    if b_att is not None:
                        if i == 3:
                            for h in range(2):
                                dve_stats2(dve, b_att, h)
                        if i == 5:
                            for h in range(2):
                                dve_norm2(dve, b_att, h)
                            for h in range(2):
                                dve_norm2_lo(dve, b_att, h)
                            dve_first(dve, b_att)
                        if i == 6:
                            dve_second(dve, b_att)
                    if b_next is not None:
                        if i == 10:
                            for pair in range(2):
                                dve_features(dve, b_next, pair)
                        if i == 13:
                            dve_den(dve, b_next, 1)
                        if i == 14:
                            for h in range(2):
                                dve_qs(dve, b_next, h)
                dve_y_copy(dve, b, 1)
                dve_out(dve, b, 1)

            dve.wait_ge(x_in[0], 16)
            for j in halves[0]:
                nc.vector.bn_stats(parts[:, j, :], x_sb[:, token_cols(0, j, 1)])
            dve.wait_ge(x_in0_rest, 16)
            dve_stats(0, halves[1])
            moments1(0)
            for half in range(2):
                dve_norm1(dve, 0, half)
            stats1(1)
            moments1(1)
            stats1(2)
            for pair in range(2):
                dve_features(dve, 0, pair)
            moments1(2)
            stats1(3)
            for h in range(2):
                dve_den(dve, 0, h)
                dve_rden(dve, 0, h)
                dve_qs(dve, 0, h)
                if h == 0:
                    dve.wait_ge(s["consts"], 1)
                    dve_kvT(dve, 0)
            dve_norm1(dve, 1, 0)
            moments1(3)
            for h in range(2):
                dve_x1(dve, 0, h)
                wait_apart(dve, "x1_done", h + 1)
                dve_stats(0, halves[h])
                if h == 0:
                    wait_apart(dve, "ln1_rstd_done", B)
                    wait_apart(dve, "ln1_mean_done", B)
                dve_moments(dve, B + h, halves[h])
                if h == 0:
                    dve_norm1(dve, 1, 1)
            for h in range(2):
                dve_norm2(dve, 0, h)
            dve_features(dve, 1, 0)
            for h in range(2):
                dve_norm2_lo(dve, 0, h)
            dve_features(dve, 1, 1)
            dve_first(dve, 0)
            dve_second(dve, 0)
            dve_combine(dve, 0)
            dve_kvT(dve, 1)
            for i in range(AHEAD):
                dve_weigh(dve, 0, i)
            for i in range(AHEAD - 1):
                dve_hidden_lo(dve, 0, i)
            for h in range(2):
                dve_den(dve, 1, h)
            for h in range(2):
                dve_rden(dve, 1, h)
            for h in range(2):
                dve_qs(dve, 1, h)
            with dve.Fori(1, B - 1) as b:
                experts(b - 1, b, b + 1, True)
            experts(B - 2, B - 1, None, True)
            experts(B - 1, None, None, False)

        @block.tensor
        def _(pe):
            start_count(pe, "y_done")
            start_count(pe, "outT_done")

            def experts(b, b_att, b_next, more):
                for i in range(STEPS):
                    ahead(pe_hidden, pe, b, i, more)
                    if i == 9:
                        pe_out_transposed(pe, b, 0, b_att, b_next)
                    if b_att is not None:
                        if i == 1:
                            for h in range(2):
                                pe_qs_transposed(pe, b_att, h)
                        if i == 6:
                            for h in range(2):
                                pe_norm2_transposed(pe, b_att, h)
                            for h in range(2):
                                pe_router(pe, b_att, h)
                    if b_next is not None:
                        if i == 10:
                            pe_queries_keys(pe, b_next, 0)
                        if i == 11:
                            pe_queries_keys(pe, b_next, 3)
                        if i == 12:
                            for h in range(2):
                                pe_key_tokens(pe, b_next, h)
                            pe_key_sum(pe, b_next)
                    pe_output(pe, b, i)
                    if b_att is not None:
                        if i == 1:
                            pe_project(pe, b_att, 0)
                        if i == 2:
                            pe_project(pe, b_att, 1)
                        if i == 8:
                            pe_combine_transposed(pe, b_att)
                    if b_next is not None:
                        if i == 9:
                            for h in range(2):
                                pe_norm1_transposed(pe, b_next, h)
                        if i == 10:
                            for u in range(1, 3):
                                pe_queries_keys(pe, b_next, u)
                        if i == 12:
                            pe_kvT(pe, b_next)
                        if i == 13:
                            pe_w(pe, b_next)
                pe_out_transposed(pe, b, 1, b_att, b_next)

            pe.wait_ge(s["consts"], 1)
            pe.wait_ge(s["w_attn"], 64)
            pe_norm1_transposed(pe, 0, 0)
            pe_norm1_transposed(pe, 0, 1)
            for u in range(4):
                pe_queries_keys(pe, 0, u)
            pe_key_tokens(pe, 0, 0)
            pe_key_tokens(pe, 0, 1)
            pe_kvT(pe, 0)
            pe_w(pe, 0)
            pe_qs_transposed(pe, 0, 0)
            pe_project(pe, 0, 0)
            pe_qs_transposed(pe, 0, 1)
            pe_project(pe, 0, 1)
            for h in range(2):
                pe_norm1_transposed(pe, 1, h)
            for u in range(2):
                pe_queries_keys(pe, 1, u)
            pe_norm2_transposed(pe, 0, 0)
            pe_norm2_transposed(pe, 0, 1)
            for u in range(2, 4):
                pe_queries_keys(pe, 1, u)
            pe_router(pe, 0, 0)
            pe_router(pe, 0, 1)
            for h in range(2):
                pe_key_tokens(pe, 1, h)
            pe_key_sum(pe, 1)
            pe.wait_ge(s["w1_split"], 2)
            for i in range(AHEAD):
                pe_hidden(pe, 0, i)
            pe.wait_ge(s["w2_split"], 2)
            pe_combine_transposed(pe, 0)
            pe_spread_combine(pe, 0)
            pe_kvT(pe, 1)
            pe_spread_combine(pe, 1)
            pe_w(pe, 1)
            with pe.Fori(1, B - 1) as b:
                experts(b - 1, b, b + 1, True)
            experts(B - 2, B - 1, None, True)
            experts(B - 1, None, None, False)


def kernel(L0_attn_x, L0_attn_wq, L0_attn_wk, L0_attn_wv, L0_attn_wo, L0_attn_bo,
           L0_ffn_router_w, L0_ffn_w1, L0_ffn_b1, L0_ffn_w2, L0_ffn_b2):
    import numpy as np
    import concourse.bacc as bacc
    from concourse.bass_utils import run_bass_kernel_spmd

    def c(a):
        return np.ascontiguousarray(a)

    x = np.asarray(L0_attn_x)
    E, F, D = L0_ffn_w1.shape
    FC = F // P
    arrays = {
        "x": c(x),
        "wqkT": c(np.concatenate([np.asarray(L0_attn_wq).T, np.asarray(L0_attn_wk).T], axis=1)),
        "wvT": c(np.asarray(L0_attn_wv).T),
        "woT": c(np.asarray(L0_attn_wo).T),
        "bo": c(L0_attn_bo),
        "routerT": c(np.asarray(L0_ffn_router_w).T),
        "w1T": c(np.asarray(L0_ffn_w1).transpose(2, 0, 1).reshape(D, E * F)),
        "b1T": c(np.asarray(L0_ffn_b1).reshape(E, FC, P).transpose(2, 0, 1).reshape(P, E * FC)),
        "w2T": c(np.asarray(L0_ffn_w2).reshape(E, D, FC, P).transpose(3, 0, 2, 1).reshape(P, E * FC * D)),
        "b2": c(L0_ffn_b2),
    }
    nc = bacc.Bacc("TRN2", target_bir_lowering=False, num_devices=1)
    args = [nc.dram_tensor(f"in_{n}", a.shape, mybir.dt.from_np(a.dtype), kind="ExternalInput").ap()
            for n, a in arrays.items()]
    out = nc.dram_tensor("out", x.shape, F32, kind="ExternalOutput").ap()
    attention_moe_program(nc, *args, out)
    r = run_bass_kernel_spmd(nc, [{f"in_{n}": a for n, a in arrays.items()}], core_ids=[0])
    return r.results[0]["out"]
```
